# Optimizing a Trainium2 kernel written in Bass

```python
import numpy as np
import jax
import jax.numpy as jnp

def _softmax(x, axis=-1):
    return jax.nn.softmax(x, axis=axis)

def _gelu(x):
    return jax.nn.gelu(x, approximate=True)

def _silu(x):
    return jax.nn.silu(x)

def _sigmoid(x):
    return jax.nn.sigmoid(x)

def _layernorm(x, axis=-1, eps=1e-05):
    m = jnp.mean(x, axis=axis, keepdims=True)
    v = jnp.var(x, axis=axis, keepdims=True)
    return (x - m) / jnp.sqrt(v + eps)

def _scatter_add(tgt, idx, src, axis=0):
    return tgt.at[idx].add(src)

def _segment_sum(src, seg, n):
    return jax.ops.segment_sum(src, seg, n)
kernel_name = 'mk_conv_seq_d1_conv_nchw256_r2_398f8d'

def setup_inputs(seed: int=0):
    np.random.seed(seed)
    _w = jnp.asarray

    def _rec_inputs():
        import jax
        import jax.numpy as jnp
        _gk = jax.random.key(seed)
        x = -0.0002928 + 1 * jax.random.normal(jax.random.fold_in(_gk, 1), (4, 128, 32, 32), jnp.float32)
        return x
    x = _rec_inputs()

    def _L0_conv_setup():
        import jax, jax.numpy as jnp
        import numpy as np
        EPS = 1e-05
        N_GROUPS = 4
        key = jax.random.key(seed)
        ks = jax.random.split(key, 4)
        B, C, H, W = (4, 128, 32, 32)
        x = jax.random.normal(ks[0], (B, C, H, W), dtype=jnp.float32)
        gn_gamma = jnp.ones((C,), dtype=jnp.float32)
        gn_beta = jnp.zeros((C,), dtype=jnp.float32)
        w_qkv = jax.random.normal(ks[1], (3 * C, C), dtype=jnp.float32) / np.sqrt(C)
        b_qkv = jnp.zeros((3 * C,), dtype=jnp.float32)
        w_out = jax.random.normal(ks[2], (C, C), dtype=jnp.float32) / np.sqrt(C)
        b_out = jnp.zeros((C,), dtype=jnp.float32)
        return {'x': x, 'gn_gamma': gn_gamma, 'gn_beta': gn_beta, 'w_qkv': w_qkv, 'b_qkv': b_qkv, 'w_out': w_out, 'b_out': b_out}
    _L0_conv_all = _L0_conv_setup()
    _L0_conv_in = {k: v for k, v in _L0_conv_all.items() if k in ('gn_gamma', 'gn_beta', 'w_qkv', 'b_qkv', 'w_out', 'b_out')}
    del _L0_conv_all
    return {'x': x, 'L0_conv_gn_gamma': _L0_conv_in['gn_gamma'], 'L0_conv_gn_beta': _L0_conv_in['gn_beta'], 'L0_conv_w_qkv': _L0_conv_in['w_qkv'], 'L0_conv_b_qkv': _L0_conv_in['b_qkv'], 'L0_conv_w_out': _L0_conv_in['w_out'], 'L0_conv_b_out': _L0_conv_in['b_out']}

def reference(x, L0_conv_gn_gamma, L0_conv_gn_beta, L0_conv_w_qkv, L0_conv_b_qkv, L0_conv_w_out, L0_conv_b_out):
    import jax
    import jax.numpy as jnp

    def _L0_conv_ref(x, gn_gamma, gn_beta, w_qkv, b_qkv, w_out, b_out):
        import jax, jax.numpy as jnp
        import numpy as np
        EPS = 1e-05
        N_GROUPS = 4
        B, C, H, W = x.shape
        N = H * W
        xg = x.reshape(B, N_GROUPS, C // N_GROUPS, H, W)
        mu = xg.mean(axis=(2, 3, 4), keepdims=True)
        var = xg.var(axis=(2, 3, 4), keepdims=True)
        y = ((xg - mu) * jax.lax.rsqrt(var + EPS)).reshape(B, C, H, W)
        y = y * gn_gamma[None, :, None, None] + gn_beta[None, :, None, None]
        qkv = jnp.einsum('bchw,dc->bdhw', y, w_qkv) + b_qkv[None, :, None, None]
        q, k, v = jnp.split(qkv, 3, axis=1)
        q = q.reshape(B, C, N).transpose(0, 2, 1)
        k = k.reshape(B, C, N)
        v = v.reshape(B, C, N).transpose(0, 2, 1)
        scores = jnp.einsum('bnc,bcm->bnm', q, k) * C ** (-0.5)
        w = jax.nn.softmax(scores, axis=-1)
        a = jnp.einsum('bnm,bmc->bnc', w, v)
        a = a.transpose(0, 2, 1).reshape(B, C, H, W)
        out = jnp.einsum('bchw,dc->bdhw', a, w_out) + b_out[None, :, None, None]
        return x + out

    def _gn(v, G=32, eps=1e-05):
        B_, C_, H_, W_ = v.shape
        g = v.reshape(B_, G, C_ // G, H_, W_)
        m = jnp.mean(g, axis=(2, 3, 4), keepdims=True)
        s = jnp.var(g, axis=(2, 3, 4), keepdims=True)
        return ((g - m) / jnp.sqrt(s + eps)).reshape(v.shape)

    def _ln_c(v, eps=1e-06):
        m = jnp.mean(v, axis=1, keepdims=True)
        s = jnp.var(v, axis=1, keepdims=True)
        return (v - m) / jnp.sqrt(s + eps)

    def _ln_t(v, eps=1e-05):
        m = jnp.mean(v, axis=-1, keepdims=True)
        s = jnp.var(v, axis=-1, keepdims=True)
        return (v - m) / jnp.sqrt(s + eps)

    def _to_tokens(v):
        B_, C_, H_, W_ = v.shape
        return v.reshape(B_, C_, H_ * W_).transpose(0, 2, 1)

    def _from_tokens(t, like):
        B_, C_, H_, W_ = like.shape
        return t.transpose(0, 2, 1).reshape(B_, C_, H_, W_)
    x = _L0_conv_ref(x, L0_conv_gn_gamma, L0_conv_gn_beta, L0_conv_w_qkv, L0_conv_b_qkv, L0_conv_w_out, L0_conv_b_out)
    return x

_drawn_inputs = setup_inputs


def setup_inputs(seed=0):
    import zlib

    import numpy as np

    out = dict(_drawn_inputs(seed))
    spreads = {'L0_conv_gn_gamma': (1.0, 0.2),
     'L0_conv_gn_beta': (0.0, 0.1),
     'L0_conv_b_qkv': (0.0, 0.1),
     'L0_conv_b_out': (0.0, 0.1)}
    factors = {}
    for name, (base, spread) in spreads.items():
        noise = np.random.default_rng([zlib.crc32(name.encode()), seed]).standard_normal(out[name].shape)
        drawn = base * np.exp(spread * noise) if base else spread * noise
        out[name] = jnp.asarray(drawn.astype(out[name].dtype))
    for name, factor in factors.items():
        out[name] = (out[name] * factor).astype(out[name].dtype)
    return out
```

```python
import concourse.bass as bass
from concourse import mybir
from contextlib import ExitStack


def attention_kernel(nc, x, gamma, beta, w_qkv, b_qkv, w_out, b_out, out):
    fp32 = mybir.dt.float32
    fp32r = mybir.dt.float32r
    ALU = mybir.AluOpType
    ACT = mybir.ActivationFunctionType
    AX = mybir.AxisListType

    BATCHES, C, H, W = x.shape
    N = H * W
    GROUPS = 4
    CG = C // GROUPS
    EPS = 1e-5
    SCALE = float(C) ** -0.5
    HALF = 512
    HALVES = N // HALF
    BLOCKS = N // 128
    QB = HALF // 128
    KB = HALF // 128
    PAIR = BLOCKS // QB
    PJ = 6
    K0, K1, Q0, Q1, VA, VB = range(PJ)
    RING = 4

    x_v = x.rearrange("b c h w -> b c (h w)")
    out_v = out.rearrange("b c h w -> b c (h w)")

    ctx = ExitStack()
    with ctx:
        def sb(name, shape, dt=fp32):
            return ctx.enter_context(nc.sbuf_tensor(name, shape, dt))

        def ps(name, shape):
            return ctx.enter_context(nc.psum_tensor(name, shape, fp32))

        def sem(name):
            return ctx.enter_context(nc.semaphore(name))

        xs = sb("xs", [C, BATCHES * N])
        wqkv = sb("wqkv", [128, 3, C])
        wout = sb("wout", [128, C])
        vec_rows = sb("vec_rows", [6, C])
        vecs = sb("vecs", [C, 6])
        GAMMA, BETA, BQ, BK, BV, BOUT = (vecs[:, i:i + 1] for i in range(6))
        ident = sb("ident", [128, 128])
        group_mean = sb("group_mean", [128, 128])
        minus_half = sb("minus_half", [128, BATCHES])
        wq_hi, wq_lo = sb("wq_hi", [C, C], fp32r), sb("wq_lo", [C, C], fp32r)
        wk_hi, wk_lo = sb("wk_hi", [C, C], fp32r), sb("wk_lo", [C, C], fp32r)
        wout_t = sb("wout_t", [C, C])
        wv_out = sb("wv_out", [C, C])
        bq_scaled = sb("bq_scaled", [C, 1])
        out_bias = sb("out_bias", [C, 1])
        stats = sb("stats", [C, BATCHES * HALVES, 6])
        mean_var = sb("mean_var", [C, BATCHES, 2])
        dev = sb("dev", [C, BATCHES])
        spread = sb("spread", [C, BATCHES])
        var_eps = sb("var_eps", [C, BATCHES])
        rstd = sb("rstd", [C, BATCHES])
        norm_a = sb("norm_a", [C, BATCHES])
        shift = sb("shift", [C, BATCHES])
        norm_b = sb("norm_b", [C, BATCHES])
        y = sb("y", [C, N])
        y_hi, y_lo = sb("y_hi", [C, N], fp32r), sb("y_lo", [C, N], fp32r)
        y_keys = sb("y_keys", [C, N])
        q_hi, q_lo = sb("q_hi", [C, N], fp32r), sb("q_lo", [C, N], fp32r)
        k_hi, k_lo = sb("k_hi", [C, 2 * N], fp32r), sb("k_lo", [C, 2 * N], fp32r)
        v_hi, v_lo = sb("v_hi", [128, N], fp32r), sb("v_lo", [128, N], fp32r)
        neg_max = sb("neg_max", [128, BLOCKS])
        row_sum = sb("row_sum", [128, BLOCKS])
        inv_sum = sb("inv_sum", [128, BLOCKS])
        probs = sb("probs", [128, RING, N])
        pt_hi = sb("pt_hi", [128, 2, BLOCKS, HALF], fp32r)
        pt_lo = sb("pt_lo", [128, 2, BLOCKS, HALF], fp32r)
        result = sb("result", [C, 2, HALF])

        scores = ps("scores", [128, 2, N])
        turned = ps("turned", [128, 2, HALF])
        mixed = ps("mixed", [C, HALF])
        projected = ps("projected", [128, HALF])

        s_x = [sem(f"x_loaded{b}") for b in range(BATCHES)]
        s_w = sem("weights_loaded")
        s_vecs = sem("vectors_loaded")
        s_vecs_turned = sem("vectors_turned")
        s_vecs_ready = sem("vectors_ready")
        s_const = sem("constants_made")
        s_stat = sem("stats_step")
        s_gmean = sem("group_sums_ready")
        s_rstd = sem("rstd_ready")
        s_norm = sem("norm_ready")
        s_wt = sem("weights_turned")
        s_wt_hi = sem("weight_heads_ready")
        s_wt_done = sem("weights_evacuated")
        s_y = sem("y_ready")
        s_y_hi = sem("y_head_ready")
        s_y_lo = sem("y_tail_ready")
        s_y_keys = sem("y_keys_ready")
        s_pj = sem("projected_ready")
        s_pj_hi = sem("projection_head_ready")
        s_pj_lo = sem("projection_tail_ready")
        s_scores = sem("scores_ready")
        s_max = sem("max_ready")
        s_exp = sem("exp_ready")
        s_inv = sem("inv_sum_ready")
        s_probs = sem("probs_normalised")
        s_turned = sem("probs_turned")
        s_pt_hi = sem("turned_head_ready")
        s_pt_lo = sem("turned_tail_ready")
        s_mixed = sem("mixed_chunk_done")
        s_result = sem("result_ready")
        s_stored = [sem("stored_even"), sem("stored_odd")]
        s_pool = sem("pool_go")

        block_ctx = ctx.enter_context(nc.Block())

        def wait(eng, s, value):
            if isinstance(value, int) and value <= 0:
                return
            eng.wait_ge(s, value)

        @block_ctx.sync
        def _(sp):
            for h in range(HALVES):
                sp.dma_start(xs[:, h * HALF:(h + 1) * HALF],
                             x_v[0, :, h * HALF:(h + 1) * HALF]).then_inc(s_x[0], 16)
            sp.dma_start(wqkv[:, :, :], w_qkv.rearrange("(t p) c -> p t c", p=128)).then_inc(s_w, 16)
            sp.dma_start(wout[:, :], w_out).then_inc(s_w, 16)
            for b in range(1, BATCHES):
                sp.dma_start(xs[:, b * N:(b + 1) * N], x_v[b]).then_inc(s_x[b], 16)

            def store(b, g):
                sp.wait_ge(s_result, PAIR_GROUPS * b + g + 1)
                sp.dma_start(out_v[b, :, g * HALF:(g + 1) * HALF] if isinstance(b, int) else
                             out_v[bass.ds(b, 1), :, g * HALF:(g + 1) * HALF].rearrange("b c n -> (b c) n"),
                             result[:, g, :]).then_inc(s_stored[g], 16)

            with sp.Fori(0, BATCHES) as b:
                for g in range(PAIR_GROUPS):
                    store(b, g)
            for g in range(PAIR_GROUPS):
                sp.wait_ge(s_stored[g], 16 * BATCHES)

        @block_ctx.gpsimd
        def _(pool):
            pool.memset(ident[:, :], 0.0).then_inc(s_const, 1)
            pool.memset(group_mean[:, :], 0.0).then_inc(s_const, 1)
            pool.memset(minus_half[:, :], -0.5).then_inc(s_const, 1)
            pool.wait_ge(s_const, 3)
            pool.affine_select(out=ident[:, :], in_=ident[:, :], compare_op=ALU.not_equal, fill=1.0,
                               base=0, pattern=[[-1, 128]], channel_multiplier=1).then_inc(s_const, 1)
            for g in range(GROUPS):
                pool.wait_ge(s_const, 4 + g)
                pool.memset(group_mean[g * CG:(g + 1) * CG, g * CG:(g + 1) * CG], 1.0 / CG).then_inc(s_const, 1)

            def rstd_of(lo, hi, n):
                pool.wait_ge(s_stat, n)
                pool.tensor_tensor(rstd[:, lo:hi], var_eps[:, lo:hi], minus_half[:, lo:hi],
                                   ALU.pow).then_inc(s_rstd, 1)

            def y_tail(c):
                pool.wait_ge(s_y_hi, c + 1)
                if not isinstance(c, int) or c >= 1:
                    pool.wait_ge(s_pj, PJ * c - PJ + Q1 + 1)
                pool.tensor_tensor(y_lo[:, :], y[:, :], y_hi[:, :].bitcast(fp32),
                                   ALU.subtract).then_inc(s_y_lo, 1)

            def normalise(b, i):
                pool.wait_ge(s_inv, BLOCKS * b + i + 1)
                pool.sem_inc(s_pool, 1)
                pool.tensor_scalar(probs[:, i % RING, :], probs[:, i % RING, :], inv_sum[:, i:i + 1], 1.0,
                                   ALU.mult, ALU.mult).then_inc(s_probs, 1)

            rstd_of(0, 1, STAT_VAR_FIRST)
            y_tail(0)
            rstd_of(1, BATCHES, STAT_VAR_REST)
            normalise(0, 0)
            normalise(0, 1)

            def steps(b, lo, hi, last=False):
                for i in range(lo, hi):
                    if i + 2 < BLOCKS:
                        normalise(b, i + 2)
                    elif not last:
                        normalise(b + 1, i + 2 - BLOCKS)
                    if i == 1:
                        y_tail(b + 1)

            steps(0, 0, QB)
            with pool.Fori(0, BATCHES - 1) as b:
                steps(b, QB, BLOCKS)
                steps(b + 1, 0, QB)
            steps(BATCHES - 1, QB, BLOCKS, last=True)

        @block_ctx.scalar
        def _(act):
            row = 0
            for v in (gamma, beta, b_qkv, b_out):
                rows = v.shape[0] // C
                act.dma_start(vec_rows[row:row + rows, :],
                              v.rearrange("(t c) -> t c", c=C)).then_inc(s_vecs, 16)
                row += rows

            def y_head(c):
                act.wait_ge(s_y, c + 1)
                if not isinstance(c, int) or c >= 1:
                    act.wait_ge(s_pj, PJ * c - PJ + Q1 + 1)
                act.activation(y_hi[:, :], y[:, :], ACT.Copy).then_inc(s_y_hi, 1)

            def keep_y(c):
                act.wait_ge(s_y, c + 1)
                if not isinstance(c, int) or c >= 1:
                    act.wait_ge(s_pj, PJ * c)
                act.activation(y_keys[:, :], y[:, :], ACT.Copy).then_inc(s_y_keys, 1)

            def projection_head(c, p):
                act.wait_ge(s_pj, PJ * c + p + 1)
                if p in (K0, K1):
                    half = bass.ds(c % 2 * N + (p - K0) * HALF, HALF)
                    act.activation(k_hi[:, half], projected[:, :], ACT.Identity, bias=BK).then_inc(s_pj_hi, 1)
                elif p in (Q0, Q1):
                    half = bass.ds((p - Q0) * HALF, HALF)
                    act.activation(q_hi[:, half], projected[:, :], ACT.Identity,
                                   bias=bq_scaled[:, :]).then_inc(s_pj_hi, 1)
                else:
                    half = bass.ds((p - VA) * HALF, HALF)
                    act.activation(v_hi[:, half], projected[:, :], ACT.Copy).then_inc(s_pj_hi, 1)

            def exponentials(b, i):
                act.wait_ge(s_max, BLOCKS * b + i + 1)
                wait(act, s_turned, 2 * (BLOCKS * b + i - RING + 1))
                act.activation(probs[:, i % RING, :], scores[:, i % 2, :], ACT.Exp,
                               bias=neg_max[:, i:i + 1], accum_out=row_sum[:, i:i + 1]).then_inc(s_exp, 1)

            def turned_heads(b, i):
                g = i // QB
                if i % QB == 0:
                    wait(act, s_mixed, QB * (PAIR_GROUPS * b + g - 1))
                for j in range(2):
                    act.wait_ge(s_turned, 2 * (BLOCKS * b + i) + j + 1)
                    act.activation(pt_hi[:, g, j * KB:(j + 1) * KB, i % QB * 128:(i % QB + 1) * 128],
                                   turned[:, j, :].rearrange("p (k n) -> p k n", k=KB),
                                   ACT.Copy).then_inc(s_pt_hi, 1)

            act.wait_ge(s_wt, 1)
            act.activation(wq_hi[:, :], turned[:, 0, 0:C], ACT.Copy, scale=SCALE).then_inc(s_wt_hi, 1)
            act.wait_ge(s_wt, 2)
            act.activation(wk_hi[:, :], turned[:, 1, 0:C], ACT.Copy).then_inc(s_wt_hi, 1)
            y_head(0)
            act.wait_ge(s_wt_done, 3)
            keep_y(0)
            for p in (K0, K1, Q0):
                projection_head(0, p)
            exponentials(0, 0)
            projection_head(0, Q1)
            exponentials(0, 1)

            def steps(b, lo, hi, last=False):
                for i in range(lo, hi):
                    turned_heads(b, i)
                    if i + 2 < BLOCKS:
                        exponentials(b, i + 2)
                    elif not last:
                        exponentials(b + 1, i + 2 - BLOCKS)
                    if i == 0:
                        y_head(b + 1)
                    if i == 2:
                        projection_head(b, VA)
                    if i == 3:
                        projection_head(b, VB)
                    if not last:
                        if i == 4:
                            projection_head(b + 1, K0)
                            projection_head(b + 1, K1)
                        if i == 5:
                            projection_head(b + 1, Q0)
                            keep_y(b + 1)
                        if i == 7:
                            projection_head(b + 1, Q1)

            steps(0, 0, QB)
            with act.Fori(0, BATCHES - 1) as b:
                steps(b, QB, BLOCKS)
                steps(b + 1, 0, QB)
            steps(BATCHES - 1, QB, BLOCKS, last=True)

        @block_ctx.vector
        def _(dve):
            steps_done = [0]

            def link(ins):
                steps_done[0] += 1
                ins.then_inc(s_stat, 1)
                dve.wait_ge(s_stat, steps_done[0])

            def channel_stats(b):
                dve.wait_ge(s_x[b], 32 if b == 0 else 16)
                for h in range(HALVES):
                    link(dve.bn_stats(stats[:, b * HALVES + h, :],
                                      xs[:, b * N + h * HALF:b * N + (h + 1) * HALF]))
                link(dve.bn_aggr(mean_var[:, b, :], stats[:, b * HALVES:(b + 1) * HALVES, :]
                                 .rearrange("p a k -> p (a k)")))

            def group_norm(lo, hi, n):
                gm, gv = projected[:, lo:hi], projected[:, 8 + lo:8 + hi]
                dve.wait_ge(s_gmean, n)
                link(dve.tensor_tensor(dev[:, lo:hi], mean_var[:, lo:hi, 0], gm, ALU.subtract))
                link(dve.tensor_tensor(spread[:, lo:hi], dev[:, lo:hi], dev[:, lo:hi], ALU.mult))
                link(dve.tensor_tensor(spread[:, lo:hi], spread[:, lo:hi], mean_var[:, lo:hi, 1], ALU.add))
                dve.wait_ge(s_gmean, n + 1)
                link(dve.tensor_scalar(var_eps[:, lo:hi], gv, EPS, None, ALU.add))
                assert steps_done[0] == (STAT_VAR_FIRST if lo == 0 else STAT_VAR_REST)
                dve.wait_ge(s_rstd, (n + 1) // 2)
                if lo == 0:
                    dve.wait_ge(s_vecs_turned, 1)
                    dve.tensor_copy(vecs[:, :], mixed[:, C:C + 6]).then_inc(s_vecs_ready, 1)
                    dve.wait_ge(s_vecs_ready, 1)
                link(dve.tensor_scalar(norm_a[:, lo:hi], rstd[:, lo:hi], GAMMA, None, ALU.mult))
                link(dve.tensor_tensor(shift[:, lo:hi], norm_a[:, lo:hi], gm, ALU.mult))
                dve.tensor_scalar(norm_b[:, lo:hi], shift[:, lo:hi], -1.0, BETA,
                                  ALU.mult, ALU.add).then_inc(s_norm, 1)
                dve.wait_ge(s_norm, (n + 1) // 2)

            def normalised(c, source):
                if not isinstance(c, int) or c >= 1:
                    dve.wait_ge(s_y_lo, c)
                    dve.wait_ge(s_y_keys, c)
                dve.tensor_scalar(y[:, :], xs[:, bass.ds(source * N, N)], norm_a[:, bass.ds(source, 1)],
                                  norm_b[:, bass.ds(source, 1)], ALU.mult, ALU.add).then_inc(s_y, 1)

            def projection_tail(c, p):
                dve.wait_ge(s_pj_hi, PJ * c + p + 1)
                if p in (K0, K1):
                    half = bass.ds(c % 2 * N + (p - K0) * HALF, HALF)
                    dve.scalar_tensor_tensor(out=k_lo[:, half], in0=projected[:, :], scalar=BK,
                                             in1=k_hi[:, half].bitcast(fp32), op0=ALU.add,
                                             op1=ALU.subtract).then_inc(s_pj_lo, 1)
                elif p in (Q0, Q1):
                    half = bass.ds((p - Q0) * HALF, HALF)
                    dve.scalar_tensor_tensor(out=q_lo[:, half], in0=projected[:, :], scalar=bq_scaled[:, :],
                                             in1=q_hi[:, half].bitcast(fp32), op0=ALU.add,
                                             op1=ALU.subtract).then_inc(s_pj_lo, 1)
                else:
                    half = bass.ds((p - VA) * HALF, HALF)
                    dve.tensor_tensor(v_lo[:, half], projected[:, :], v_hi[:, half].bitcast(fp32),
                                      ALU.subtract).then_inc(s_pj_lo, 1)

            def maximum(b, i):
                dve.wait_ge(s_scores, BLOCKS * b + i + 1)
                dve.tensor_reduce(neg_max[:, i:i + 1], scores[:, i % 2, :], AX.X, ALU.max,
                                  negate=True).then_inc(s_max, 1)

            def inverse_sum(b, i):
                dve.wait_ge(s_exp, BLOCKS * b + i + 1)
                dve.reciprocal(inv_sum[:, i:i + 1], row_sum[:, i:i + 1]).then_inc(s_inv, 1)

            def turned_tails(b, i):
                g = i // QB
                for j in range(2):
                    dve.wait_ge(s_pt_hi, 2 * (BLOCKS * b + i) + j + 1)
                    at = (slice(None), g, slice(j * KB, (j + 1) * KB), slice(i % QB * 128, (i % QB + 1) * 128))
                    dve.tensor_tensor(pt_lo[at], turned[:, j, :].rearrange("p (k n) -> p k n", k=KB),
                                      pt_hi[at].bitcast(fp32), ALU.subtract).then_inc(s_pt_lo, 1)

            def results(b, g):
                group = PAIR_GROUPS * b + g
                dve.wait_ge(s_mixed, QB * (group + 1))
                if not isinstance(b, int) or b >= 1:
                    dve.wait_ge(s_stored[g], 16 * b)
                dve.scalar_tensor_tensor(out=result[:, g, :], in0=mixed[:, :], scalar=out_bias[:, :],
                                         in1=xs[:, bass.ds(b * N + g * HALF, HALF)], op0=ALU.add,
                                         op1=ALU.add).then_inc(s_result, 1)

            channel_stats(0)
            group_norm(0, 1, 1)
            normalised(0, 0)
            dve.wait_ge(s_wt_hi, 1)
            dve.scalar_tensor_tensor(out=wq_lo[:, :], in0=turned[:, 0, 0:C], scalar=SCALE,
                                     in1=wq_hi[:, :].bitcast(fp32), op0=ALU.mult,
                                     op1=ALU.subtract).then_inc(s_wt_done, 1)
            dve.wait_ge(s_wt_hi, 2)
            dve.tensor_tensor(wk_lo[:, :], turned[:, 1, 0:C], wk_hi[:, :].bitcast(fp32),
                              ALU.subtract).then_inc(s_wt_done, 1)
            dve.tensor_scalar(bq_scaled[:, :], BQ, SCALE, None, ALU.mult).then_inc(s_wt_done, 1)
            dve.wait_ge(s_wt, 3)
            dve.tensor_copy(wout_t[:, :], mixed[:, 0:C]).then_inc(s_wt_done, 1)
            for p in (K0, K1, Q0):
                projection_tail(0, p)
            dve.wait_ge(s_wt, 4)
            dve.tensor_copy(wv_out[:, :], scores[:, 1, 0:C]).then_inc(s_wt_done, 1)
            dve.tensor_tensor(out_bias[:, :], scores[:, 1, C:C + 1], BOUT, ALU.add).then_inc(s_wt_done, 1)
            maximum(0, 0)
            projection_tail(0, Q1)
            inverse_sum(0, 0)
            maximum(0, 1)
            for b in range(1, BATCHES):
                channel_stats(b)
            inverse_sum(0, 1)
            group_norm(1, BATCHES, 3)

            def steps(b, lo, hi, last=False):
                for i in range(lo, hi):
                    ahead = (b, i + 2) if i + 2 < BLOCKS else (b + 1, i + 2 - BLOCKS)
                    if i + 2 < BLOCKS or not last:
                        maximum(*ahead)
                    turned_tails(b, i)
                    if i + 2 < BLOCKS or not last:
                        inverse_sum(*ahead)
                    if i == 0:
                        normalised(b + 1, (b + 1) % BATCHES)
                    if i == 2:
                        projection_tail(b, VA)
                    if i == 3:
                        projection_tail(b, VB)
                        if not isinstance(b, int) or b >= 1:
                            results(b - 1, 1)
                    if not last:
                        if i == 4:
                            projection_tail(b + 1, K0)
                            projection_tail(b + 1, K1)
                        if i == 5:
                            projection_tail(b + 1, Q0)
                        if i == 7:
                            projection_tail(b + 1, Q1)
                    if i == 7:
                        results(b, 0)

            steps(0, 0, QB)
            with dve.Fori(0, BATCHES - 1) as b:
                steps(b, QB, BLOCKS)
                steps(b + 1, 0, QB)
            steps(BATCHES - 1, QB, BLOCKS, last=True)
            results(BATCHES - 1, 1)

        @block_ctx.tensor
        def _(pe):
            def group_sums(lo, hi, stat_mean, stat_var):
                pe.wait_ge(s_stat, stat_mean)
                pe.matmul(projected[:, lo:hi], group_mean[:, :], mean_var[:, lo:hi, 0],
                          start=True, stop=True).then_inc(s_gmean, 1)
                pe.wait_ge(s_stat, stat_var)
                pe.matmul(projected[:, 8 + lo:8 + hi], group_mean[:, :], spread[:, lo:hi],
                          start=True, stop=True).then_inc(s_gmean, 1)

            def split_product(to, w_hi, w_lo, m_hi, m_lo):
                pe.matmul(to, w_hi, m_hi, start=True, stop=False)
                pe.matmul(to, w_hi, m_lo, start=False, stop=False)
                return pe.matmul(to, w_lo, m_hi, start=False, stop=True)

            def projection(c, p):
                wait(pe, s_pj_lo, PJ * c + p)
                if p == K0:
                    pe.wait_ge(s_y_lo, c + 1)
                if p in (K0, K1, Q0, Q1):
                    h = (p - K0) % 2
                    w_hi, w_lo = (wk_hi, wk_lo) if p in (K0, K1) else (wq_hi, wq_lo)
                    half = slice(h * HALF, (h + 1) * HALF)
                    mm = split_product(projected[:, :], w_hi[:, :], w_lo[:, :], y_hi[:, half], y_lo[:, half])
                else:
                    if p == VA:
                        pe.wait_ge(s_y_keys, c + 1)
                    for j in range(KB):
                        key = ((p - VA) * KB + j) * 128
                        mm = pe.matmul(projected[:, j * 128:(j + 1) * 128], y_keys[:, key:key + 128],
                                       wv_out[:, :], start=True, stop=True)
                mm.then_inc(s_pj, 1)

            def block_scores(b, i):
                if i == 0:
                    pe.wait_ge(s_pj_lo, PJ * b + Q0 + 1)
                if i == QB:
                    pe.wait_ge(s_pj_lo, PJ * b + Q1 + 1)
                wait(pe, s_exp, BLOCKS * b + i - 1)
                query = slice(i * 128, (i + 1) * 128)
                keys = [bass.ds(b % 2 * N + h * HALF, HALF) for h in range(HALVES)]
                to = [scores[:, i % 2, h * HALF:(h + 1) * HALF] for h in range(HALVES)]
                for h in range(HALVES):
                    pe.matmul(to[h], q_hi[:, query], k_hi[:, keys[h]], start=True, stop=False)
                    pe.matmul(to[h], q_hi[:, query], k_lo[:, keys[h]], start=False, stop=False)
                for h in range(HALVES):
                    mm = pe.matmul(to[h], q_lo[:, query], k_hi[:, keys[h]], start=False, stop=True)
                mm.then_inc(s_scores, 1)

            def turn(b, i):
                pe.wait_ge(s_probs, BLOCKS * b + i + 1)
                for j in range(2):
                    wait(pe, s_pt_lo, 2 * (BLOCKS * b + i - 1) + j + 1)
                    for k in range(KB):
                        key = (j * KB + k) * 128
                        mm = pe.transpose(turned[:, j, k * 128:(k + 1) * 128],
                                          probs[:, i % RING, key:key + 128], ident[:, :])
                    mm.then_inc(s_turned, 1)

            def mix(b, g, chunk):
                group = PAIR_GROUPS * b + g
                if chunk == 0:
                    wait(pe, s_result, group)
                if chunk % 2 == 0:
                    pe.wait_ge(s_pt_lo, 2 * (QB * group + QB - 1) + chunk // 2 + 1)
                    if g == 0:
                        pe.wait_ge(s_pj_lo, PJ * b + (VA, VB)[chunk // 2] + 1)
                for k in range(PAIR * chunk, PAIR * (chunk + 1)):
                    channels = slice(k * 128, (k + 1) * 128)
                    pe.matmul(mixed[:, :], v_hi[:, channels], pt_hi[:, g, k, :], start=(k == 0), stop=False)
                    pe.matmul(mixed[:, :], v_hi[:, channels], pt_lo[:, g, k, :], start=False, stop=False)
                    mm = pe.matmul(mixed[:, :], v_lo[:, channels], pt_hi[:, g, k, :], start=False,
                                   stop=(k == BLOCKS - 1))
                mm.then_inc(s_mixed, 1)

            pe.wait_ge(s_const, 4 + GROUPS)
            pe.wait_ge(s_vecs, 64)
            pe.transpose(mixed[:, C:C + 6], vec_rows[:, :], ident[0:6, 0:6]).then_inc(s_vecs_turned, 1)
            pe.wait_ge(s_w, 32)
            pe.transpose(turned[:, 0, 0:C], wqkv[:, 0, :], ident[:, :]).then_inc(s_wt, 1)
            pe.transpose(turned[:, 1, 0:C], wqkv[:, 1, :], ident[:, :]).then_inc(s_wt, 1)
            pe.transpose(mixed[:, 0:C], wout[:, :], ident[:, :]).then_inc(s_wt, 1)
            group_sums(0, 1, STAT_MEAN_FIRST, STAT_VAR_FIRST - 1)
            pe.wait_ge(s_norm, 1)
            pe.wait_ge(s_wt_done, 2)
            projection(0, K0)
            projection(0, K1)
            pe.wait_ge(s_wt_done, 4)
            pe.matmul(scores[:, 1, 0:C], wqkv[:, 2, :], wout_t[:, :], start=True, stop=True)
            pe.matmul(scores[:, 1, C:C + 1], wout_t[:, :], BV, start=True, stop=True).then_inc(s_wt, 1)
            projection(0, Q0)
            block_scores(0, 0)
            projection(0, Q1)
            pe.wait_ge(s_wt_done, 6)
            block_scores(0, 1)
            pe.wait_ge(s_pj_lo, Q1 + 1)
            group_sums(1, BATCHES, STAT_MEAN_REST, STAT_VAR_REST - 1)

            def steps(b, lo, hi, last=False):
                for i in range(lo, hi):
                    if i + 2 < BLOCKS:
                        block_scores(b, i + 2)
                    elif not last:
                        block_scores(b + 1, i + 2 - BLOCKS)
                    if i == 4 and not last:
                        projection(b + 1, K0)
                    turn(b, i)
                    if i == 2:
                        if isinstance(b, int) and b == 0:
                            pe.wait_ge(s_norm, 2)
                        projection(b, VA)
                    if i >= QB:
                        mix(b, 0, i - QB)
                    elif not isinstance(b, int) or b >= 1:
                        mix(b - 1, 1, i)
                    if i == 3:
                        projection(b, VB)
                    if not last:
                        if i == 4:
                            projection(b + 1, K1)
                        if i == 5:
                            projection(b + 1, Q0)
                        if i == 7:
                            projection(b + 1, Q1)

            steps(0, 0, QB)
            with pe.Fori(0, BATCHES - 1) as b:
                steps(b, QB, BLOCKS)
                steps(b + 1, 0, QB)
            steps(BATCHES - 1, QB, BLOCKS, last=True)
            for chunk in range(QB):
                mix(BATCHES - 1, 1, chunk)


PAIR_GROUPS = 2
STAT_MEAN_FIRST = 3
STAT_VAR_FIRST = STAT_MEAN_FIRST + 4
STAT_MEAN_REST = STAT_VAR_FIRST + 2 + 3 * 3
STAT_VAR_REST = STAT_MEAN_REST + 4


_INS = ['x', 'L0_conv_gn_gamma', 'L0_conv_gn_beta', 'L0_conv_w_qkv', 'L0_conv_b_qkv', 'L0_conv_w_out',
        'L0_conv_b_out']


def kernel(**inputs):
    import numpy as _np
    import concourse.bacc as _bacc
    from concourse import mybir as _mybir
    from concourse.bass_utils import run_bass_kernel_spmd as _run

    nc = _bacc.Bacc("TRN2", target_bir_lowering=False, num_devices=1)
    arrays, args = {}, []
    for name in _INS:
        a = _np.ascontiguousarray(inputs[name])
        arrays[f"in_{name}_dram"] = a
        args.append(nc.dram_tensor(f"in_{name}_dram", a.shape, _mybir.dt.from_np(a.dtype), kind="ExternalInput").ap())
    shape = inputs['x'].shape
    args.append(nc.dram_tensor("out_0_dram", shape, _mybir.dt.float32, kind="ExternalOutput").ap())
    attention_kernel(nc, *args)
    r = _run(nc, [arrays], core_ids=[0])
    return r.results[0]["out_0_dram"]
```

```python
import concourse.bass as bass
from concourse import mybir
from contextlib import ExitStack


def attention_kernel(nc, x, vectors, weights, out):
    fp32 = mybir.dt.float32
    fp32r = mybir.dt.float32r
    ALU = mybir.AluOpType
    ACT = mybir.ActivationFunctionType
    AX = mybir.AxisListType

    BATCHES, C, H, W = x.shape
    N = H * W
    GROUPS = 4
    CG = C // GROUPS
    EPS = 1e-5
    SCALE = float(C) ** -0.5
    HALF = 512
    HALVES = N // HALF
    BLOCKS = N // 128
    QB = HALF // 128
    KB = HALF // 128
    PAIR = BLOCKS // QB
    PJ = 6
    K0, K1, Q0, Q1, VA, VB = range(PJ)
    RING = 4

    x_v = x.rearrange("b c h w -> b c (h w)")
    out_v = out.rearrange("b c h w -> b c (h w)")

    ctx = ExitStack()
    with ctx:
        def sb(name, shape, dt=fp32):
            return ctx.enter_context(nc.sbuf_tensor(name, shape, dt))

        def ps(name, shape):
            return ctx.enter_context(nc.psum_tensor(name, shape, fp32))

        def sem(name):
            return ctx.enter_context(nc.semaphore(name))

        xs = sb("xs", [C, BATCHES * N])
        vecs = sb("vecs", [C, 6])
        GAMMA, BETA, BQ, BK, BV, BOUT = (vecs[:, i:i + 1] for i in range(6))
        ws = sb("ws", [128, 4, C])
        WQ_T, WK_T, WV, WOUT_T = (ws[:, i, :] for i in range(4))
        ident = sb("ident", [128, 128])
        group_mean = sb("group_mean", [128, 128])
        minus_half = sb("minus_half", [128, BATCHES])
        wq_hi, wq_lo = sb("wq_hi", [C, C], fp32r), sb("wq_lo", [C, C], fp32r)
        wk_hi, wk_lo = sb("wk_hi", [C, C], fp32r), sb("wk_lo", [C, C], fp32r)
        wv_out = sb("wv_out", [C, C])
        bq_scaled = sb("bq_scaled", [C, 1])
        out_bias = sb("out_bias", [C, 1])
        stats = sb("stats", [C, BATCHES * HALVES, 6])
        mean_var = sb("mean_var", [C, BATCHES, 2])
        dev = sb("dev", [C, BATCHES])
        spread = sb("spread", [C, BATCHES])
        var_eps = sb("var_eps", [C, BATCHES])
        rstd = sb("rstd", [C, BATCHES])
        norm_a = sb("norm_a", [C, BATCHES])
        shift = sb("shift", [C, BATCHES])
        norm_b = sb("norm_b", [C, BATCHES])
        y = sb("y", [C, N])
        y_hi, y_lo = sb("y_hi", [C, N], fp32r), sb("y_lo", [C, N], fp32r)
        y_keys = sb("y_keys", [C, N])
        q_hi, q_lo = sb("q_hi", [C, N], fp32r), sb("q_lo", [C, N], fp32r)
        k_hi, k_lo = sb("k_hi", [C, 2 * N], fp32r), sb("k_lo", [C, 2 * N], fp32r)
        v_hi, v_lo = sb("v_hi", [128, N], fp32r), sb("v_lo", [128, N], fp32r)
        neg_max = sb("neg_max", [128, BLOCKS])
        row_sum = sb("row_sum", [128, BLOCKS])
        inv_sum = sb("inv_sum", [128, BLOCKS])
        probs = sb("probs", [128, RING, N])
        pt_hi = sb("pt_hi", [128, 2, BLOCKS, HALF], fp32r)
        pt_lo = sb("pt_lo", [128, 2, BLOCKS, HALF], fp32r)
        result = sb("result", [C, 2, HALF])

        scores = ps("scores", [128, 2, N])
        turned = ps("turned", [128, 2, HALF])
        mixed = ps("mixed", [C, HALF])
        projected = ps("projected", [128, HALF])
        FIRST_BANK = (projected, mixed, turned[:, 0, :], turned[:, 1, :])

        s_x = [sem(f"x_loaded{b}") for b in range(BATCHES)]
        s_x_half = sem("second_half_of_first_x_loaded")
        s_w = sem("weights_loaded")
        s_vecs = sem("vectors_loaded")
        s_const = sem("constants_made")
        s_step = sem("dve_step")
        s_means = sem("channel_means_ready")
        s_gmean = sem("group_means_ready")
        s_spread = sem("channel_spreads_ready")
        s_gvar = sem("group_variances_ready")
        s_var_eps = sem("variance_eps_ready")
        s_rstd = sem("rstd_ready")
        s_norm = sem("norm_ready")
        s_w_hi = sem("weight_heads_ready")
        s_w_lo = sem("weight_tails_ready")
        s_wv = sem("folded_weights_ready")
        s_wv_out = sem("folded_weights_taken")
        s_y = sem("y_ready")
        s_y_first = sem("half_of_first_y_ready")
        s_y_hi_first = sem("half_of_first_y_head_ready")
        s_y_lo_first = sem("half_of_first_y_tail_ready")
        s_y_hi = sem("y_head_ready")
        s_y_lo = sem("y_tail_ready")
        s_y_keys = sem("y_keys_ready")
        s_pj = sem("projected_ready")
        s_pj_hi = sem("projection_head_ready")
        s_pj_lo = sem("projection_tail_ready")
        s_scores = sem("scores_ready")
        s_max = sem("max_ready")
        s_exp = sem("exp_ready")
        s_inv = sem("inv_sum_ready")
        s_probs = sem("probs_normalised")
        s_turned = sem("probs_turned")
        s_pt_hi = sem("turned_head_ready")
        s_pt_lo = sem("turned_tail_ready")
        s_mixed = sem("mixed_chunk_done")
        s_result = sem("result_ready")
        s_stored = [sem("stored_even"), sem("stored_odd")]
        s_pool = sem("pool_go")

        block_ctx = ctx.enter_context(nc.Block())

        def wait(eng, s, value):
            if isinstance(value, int) and value <= 0:
                return
            eng.wait_ge(s, value)

        @block_ctx.sync
        def _(sp):
            sp.dma_start(xs[:, 0:HALF], x_v[0, :, 0:HALF]).then_inc(s_x[0], 16)
            sp.dma_start(ws[:, :, :], weights.rearrange("p (t c) -> p t c", t=4)).then_inc(s_w, 16)
            for b in range(1, BATCHES):
                sp.dma_start(xs[:, b * N:(b + 1) * N], x_v[b]).then_inc(s_x[b], 16)

            def store(b, g):
                sp.wait_ge(s_result, PAIR_GROUPS * b + g + 1)
                sp.dma_start(out_v[b, :, g * HALF:(g + 1) * HALF] if isinstance(b, int) else
                             out_v[bass.ds(b, 1), :, g * HALF:(g + 1) * HALF].rearrange("b c n -> (b c) n"),
                             result[:, g, :]).then_inc(s_stored[g], 16)

            with sp.Fori(0, BATCHES) as b:
                for g in range(PAIR_GROUPS):
                    store(b, g)
            for g in range(PAIR_GROUPS):
                sp.wait_ge(s_stored[g], 16 * BATCHES)

        @block_ctx.gpsimd
        def _(pool):
            pool.memset(ident[:, :], 0.0).then_inc(s_const, 1)
            pool.memset(group_mean[:, :], 0.0).then_inc(s_const, 1)
            pool.memset(minus_half[:, :], -0.5).then_inc(s_const, 1)
            pool.wait_ge(s_const, 3)
            pool.affine_select(out=ident[:, :], in_=ident[:, :], compare_op=ALU.not_equal, fill=1.0,
                               base=0, pattern=[[-1, 128]], channel_multiplier=1).then_inc(s_const, 1)
            for g in range(GROUPS):
                pool.wait_ge(s_const, 4 + g)
                pool.memset(group_mean[g * CG:(g + 1) * CG, g * CG:(g + 1) * CG], 1.0 / CG).then_inc(s_const, 1)

            def rstd_of(lo, hi, n):
                pool.wait_ge(s_var_eps, n)
                pool.tensor_tensor(rstd[:, lo:hi], var_eps[:, lo:hi], minus_half[:, lo:hi],
                                   ALU.pow).then_inc(s_rstd, 1)

            def y_tail(c):
                pool.wait_ge(s_y_hi, c)
                pool.tensor_tensor(y_lo[:, :], y[:, :], y_hi[:, :].bitcast(fp32),
                                   ALU.subtract).then_inc(s_y_lo, 1)

            def normalise(b, i):
                pool.wait_ge(s_inv, BLOCKS * b + i + 1)
                pool.sem_inc(s_pool, 1)
                pool.tensor_scalar(probs[:, i % RING, :], probs[:, i % RING, :], inv_sum[:, i:i + 1], 1.0,
                                   ALU.mult, ALU.mult).then_inc(s_probs, 1)

            rstd_of(0, 1, 1)
            normalise(0, 0)
            normalise(0, 1)

            def steps(b, lo, hi, last=False, first=False):
                for i in range(lo, hi):
                    if i == 3:
                        y_tail(b + 1)
                    if i + 2 < BLOCKS:
                        normalise(b, i + 2)
                    elif not last:
                        normalise(b + 1, i + 2 - BLOCKS)
                    if first and i == 1:
                        rstd_of(1, BATCHES, 2)

            steps(0, 0, QB, first=True)
            with pool.Fori(0, BATCHES - 1) as b:
                steps(b, QB, BLOCKS)
                steps(b + 1, 0, QB)
            steps(BATCHES - 1, QB, BLOCKS, last=True)

        @block_ctx.scalar
        def _(act):
            act.dma_start(xs[:, HALF:N], x_v[0, :, HALF:N]).then_inc(s_x_half, 16)
            act.dma_start(vecs[:, :], vectors).then_inc(s_vecs, 16)

            def y_head(c):
                act.wait_ge(s_y, c)
                act.wait_ge(s_pj, PJ * c - PJ + Q1 + 1)
                act.activation(y_hi[:, :], y[:, :], ACT.Copy).then_inc(s_y_hi, 1)

            def keep_y(c):
                if isinstance(c, int):
                    act.wait_ge(s_y_first, HALVES)
                else:
                    act.wait_ge(s_y, c)
                if not isinstance(c, int) or c >= 1:
                    act.wait_ge(s_pj, PJ * c)
                act.activation(y_keys[:, :], y[:, :], ACT.Copy).then_inc(s_y_keys, 1)

            def projection_head(c, p, bank=projected):
                act.wait_ge(s_pj, PJ * c + p + 1)
                bank = bank[:, 0:HALF]
                if p in (K0, K1):
                    half = bass.ds(c % 2 * N + (p - K0) * HALF, HALF)
                    act.activation(k_hi[:, half], bank, ACT.Identity, bias=BK).then_inc(s_pj_hi, 1)
                elif p in (Q0, Q1):
                    half = bass.ds((p - Q0) * HALF, HALF)
                    act.activation(q_hi[:, half], bank, ACT.Identity,
                                   bias=bq_scaled[:, :]).then_inc(s_pj_hi, 1)
                else:
                    half = bass.ds((p - VA) * HALF, HALF)
                    act.activation(v_hi[:, half], bank, ACT.Copy).then_inc(s_pj_hi, 1)

            def exponentials(b, i):
                act.wait_ge(s_max, BLOCKS * b + i + 1)
                wait(act, s_turned, 2 * (BLOCKS * b + i - RING + 1))
                act.activation(probs[:, i % RING, :], scores[:, i % 2, :], ACT.Exp,
                               bias=neg_max[:, i:i + 1], accum_out=row_sum[:, i:i + 1]).then_inc(s_exp, 1)

            def turned_heads(b, i):
                g = i // QB
                if i % QB == 0:
                    wait(act, s_mixed, QB * (PAIR_GROUPS * b + g - 1))
                for j in range(2):
                    act.wait_ge(s_turned, 2 * (BLOCKS * b + i) + j + 1)
                    act.activation(pt_hi[:, g, j * KB:(j + 1) * KB, i % QB * 128:(i % QB + 1) * 128],
                                   turned[:, j, :].rearrange("p (k n) -> p k n", k=KB),
                                   ACT.Copy).then_inc(s_pt_hi, 1)

            act.wait_ge(s_w, 16)
            act.activation(wq_hi[:, :], WQ_T, ACT.Copy, scale=SCALE).then_inc(s_w_hi, 1)
            act.activation(wk_hi[:, :], WK_T, ACT.Copy).then_inc(s_w_hi, 1)
            act.wait_ge(s_norm, 1)
            for h in range(HALVES):
                half = slice(h * HALF, (h + 1) * HALF)
                act.activation(y_hi[:, half], xs[:, half], ACT.Identity, scale=norm_a[:, 0:1],
                               bias=norm_b[:, 0:1]).then_inc(s_y_hi_first, 1)
            act.wait_ge(s_w_lo, 3)
            for p in (K0, K1, Q0, Q1):
                projection_head(0, p, FIRST_BANK[p])
            exponentials(0, 0)
            exponentials(0, 1)
            keep_y(0)

            def steps(b, lo, hi, last=False, first=False):
                for i in range(lo, hi):
                    if i == 4:
                        projection_head(b, VB)
                    if i in (5, 6) and not last:
                        projection_head(b + 1, {5: K1, 6: Q0}[i])
                    turned_heads(b, i)
                    if i == 2:
                        projection_head(b, VA)
                    if i in (4, 7) and not last:
                        projection_head(b + 1, {4: K0, 7: Q1}[i])
                    if i + 2 < BLOCKS:
                        exponentials(b, i + 2)
                    elif not last:
                        exponentials(b + 1, i + 2 - BLOCKS)
                    if i == 2:
                        y_head(b + 1)
                    if i == 4 and not last:
                        keep_y(b + 1)

            steps(0, 0, QB)
            with act.Fori(0, BATCHES - 1) as b:
                steps(b, QB, BLOCKS)
                steps(b + 1, 0, QB)
            steps(BATCHES - 1, QB, BLOCKS, last=True)

        @block_ctx.vector
        def _(dve):
            steps_done = [0]

            def step(ins):
                steps_done[0] += 1
                ins.then_inc(s_step, 1)

            def own_steps():
                dve.wait_ge(s_step, steps_done[0])

            def half_stats(b, h):
                if b > 0:
                    dve.wait_ge(s_x[b], 16)
                else:
                    dve.wait_ge((s_x[0], s_x_half)[h], 16)
                step(dve.bn_stats(stats[:, b * HALVES + h, :],
                                  xs[:, b * N + h * HALF:b * N + (h + 1) * HALF]))

            def channel_stats(lo, hi):
                own_steps()
                for b in range(lo, hi):
                    mm = dve.bn_aggr(mean_var[:, b, :], stats[:, b * HALVES:(b + 1) * HALVES, :]
                                     .rearrange("p a k -> p (a k)"))
                    mm.then_inc(s_means, 1)

            def channel_spreads(lo, hi, n, sums):
                dve.wait_ge(s_gmean, n)
                step(dve.tensor_tensor(dev[:, lo:hi], mean_var[:, lo:hi, 0], sums[:, lo:hi], ALU.subtract))
                own_steps()
                step(dve.tensor_tensor(spread[:, lo:hi], dev[:, lo:hi], dev[:, lo:hi], ALU.mult))
                own_steps()
                dve.tensor_tensor(spread[:, lo:hi], spread[:, lo:hi], mean_var[:, lo:hi, 1],
                                  ALU.add).then_inc(s_spread, 1)

            def variances(lo, hi, n, sums):
                dve.wait_ge(s_gvar, n)
                dve.tensor_scalar(var_eps[:, lo:hi], sums[:, 8 + lo:8 + hi], EPS, None,
                                  ALU.add).then_inc(s_var_eps, 1)

            def coefficients(lo, hi, n, sums):
                dve.wait_ge(s_rstd, n)
                step(dve.tensor_scalar(norm_a[:, lo:hi], rstd[:, lo:hi], GAMMA, None, ALU.mult))
                own_steps()
                step(dve.tensor_tensor(shift[:, lo:hi], norm_a[:, lo:hi], sums[:, lo:hi], ALU.mult))
                own_steps()
                dve.tensor_scalar(norm_b[:, lo:hi], shift[:, lo:hi], -1.0, BETA,
                                  ALU.mult, ALU.add).then_inc(s_norm, 1)
                dve.wait_ge(s_norm, n)

            def normalised(c, source):
                if isinstance(c, int) and c == 1:
                    dve.wait_ge(s_y_lo_first, HALVES)
                else:
                    dve.wait_ge(s_y_lo, c - 1)
                dve.wait_ge(s_y_keys, c)
                dve.tensor_scalar(y[:, :], xs[:, bass.ds(source * N, N)], norm_a[:, bass.ds(source, 1)],
                                  norm_b[:, bass.ds(source, 1)], ALU.mult, ALU.add).then_inc(s_y, 1)

            def projection_tail(c, p, bank=projected):
                dve.wait_ge(s_pj_hi, PJ * c + p + 1)
                bank = bank[:, 0:HALF]
                if p in (K0, K1):
                    half = bass.ds(c % 2 * N + (p - K0) * HALF, HALF)
                    dve.scalar_tensor_tensor(out=k_lo[:, half], in0=bank, scalar=BK,
                                             in1=k_hi[:, half].bitcast(fp32), op0=ALU.add,
                                             op1=ALU.subtract).then_inc(s_pj_lo, 1)
                elif p in (Q0, Q1):
                    half = bass.ds((p - Q0) * HALF, HALF)
                    dve.scalar_tensor_tensor(out=q_lo[:, half], in0=bank, scalar=bq_scaled[:, :],
                                             in1=q_hi[:, half].bitcast(fp32), op0=ALU.add,
                                             op1=ALU.subtract).then_inc(s_pj_lo, 1)
                else:
                    half = bass.ds((p - VA) * HALF, HALF)
                    dve.tensor_tensor(v_lo[:, half], bank, v_hi[:, half].bitcast(fp32),
                                      ALU.subtract).then_inc(s_pj_lo, 1)

            def maximum(b, i):
                dve.wait_ge(s_scores, BLOCKS * b + i + 1)
                dve.tensor_reduce(neg_max[:, i:i + 1], scores[:, i % 2, :], AX.X, ALU.max,
                                  negate=True).then_inc(s_max, 1)

            def inverse_sum(b, i):
                dve.wait_ge(s_exp, BLOCKS * b + i + 1)
                dve.reciprocal(inv_sum[:, i:i + 1], row_sum[:, i:i + 1]).then_inc(s_inv, 1)

            def turned_tails(b, i):
                g = i // QB
                for j in range(2):
                    dve.wait_ge(s_pt_hi, 2 * (BLOCKS * b + i) + j + 1)
                    at = (slice(None), g, slice(j * KB, (j + 1) * KB), slice(i % QB * 128, (i % QB + 1) * 128))
                    dve.tensor_tensor(pt_lo[at], turned[:, j, :].rearrange("p (k n) -> p k n", k=KB),
                                      pt_hi[at].bitcast(fp32), ALU.subtract).then_inc(s_pt_lo, 1)

            def results(b, g, bank=mixed):
                group = PAIR_GROUPS * b + g
                dve.wait_ge(s_mixed, QB * (group + 1))
                if not isinstance(b, int) or b >= 1:
                    dve.wait_ge(s_stored[g], 16 * b)
                dve.scalar_tensor_tensor(out=result[:, g, :], in0=bank[:, :], scalar=out_bias[:, :],
                                         in1=xs[:, bass.ds(b * N + g * HALF, HALF)], op0=ALU.add,
                                         op1=ALU.add).then_inc(s_result, 1)

            half_stats(0, 0)
            half_stats(0, 1)
            channel_stats(0, 1)
            channel_spreads(0, 1, 1, projected)
            dve.wait_ge(s_w_hi, 1)
            dve.scalar_tensor_tensor(out=wq_lo[:, :], in0=WQ_T, scalar=SCALE,
                                     in1=wq_hi[:, :].bitcast(fp32), op0=ALU.mult,
                                     op1=ALU.subtract).then_inc(s_w_lo, 1)
            variances(0, 1, 1, projected)
            dve.wait_ge(s_w_hi, 2)
            dve.tensor_tensor(wk_lo[:, :], WK_T, wk_hi[:, :].bitcast(fp32),
                              ALU.subtract).then_inc(s_w_lo, 1)
            dve.wait_ge(s_vecs, 16)
            dve.tensor_scalar(bq_scaled[:, :], BQ, SCALE, None, ALU.mult).then_inc(s_w_lo, 1)
            coefficients(0, 1, 1, projected)
            for h in range(HALVES):
                half = slice(h * HALF, (h + 1) * HALF)
                dve.tensor_scalar(y[:, half], xs[:, half], norm_a[:, 0:1], norm_b[:, 0:1],
                                  ALU.mult, ALU.add).then_inc(s_y_first, 1)
            for h in range(HALVES):
                half = slice(h * HALF, (h + 1) * HALF)
                dve.wait_ge(s_y_first, h + 1)
                dve.wait_ge(s_y_hi_first, h + 1)
                dve.tensor_tensor(y_lo[:, half], y[:, half], y_hi[:, half].bitcast(fp32),
                                  ALU.subtract).then_inc(s_y_lo_first, 1)
            dve.wait_ge(s_wv, 1)
            dve.tensor_copy(wv_out[:, :], scores[:, 1, 0:C]).then_inc(s_wv_out, 1)
            dve.tensor_tensor(out_bias[:, :], scores[:, 1, C:C + 1], BOUT, ALU.add).then_inc(s_wv_out, 1)
            half_stats(1, 0)
            half_stats(1, 1)
            projection_tail(0, K0, FIRST_BANK[K0])
            half_stats(2, 0)
            projection_tail(0, K1, FIRST_BANK[K1])
            projection_tail(0, Q0, FIRST_BANK[Q0])
            half_stats(2, 1)
            half_stats(3, 0)
            maximum(0, 0)
            projection_tail(0, Q1, FIRST_BANK[Q1])
            inverse_sum(0, 0)
            maximum(0, 1)
            half_stats(3, 1)
            inverse_sum(0, 1)
            channel_stats(1, BATCHES)

            def steps(b, lo, hi, last=False, first=False):
                for i in range(lo, hi):
                    ahead = (b, i + 2) if i + 2 < BLOCKS else (b + 1, i + 2 - BLOCKS)
                    if i == 4:
                        projection_tail(b, VB)
                    if i == 6 and not last:
                        projection_tail(b + 1, Q0)
                        turned_tails(b, i)
                    if i + 2 < BLOCKS or not last:
                        maximum(*ahead)
                    if i == 5 and not last:
                        projection_tail(b + 1, K1)
                    if i != 6 or last:
                        turned_tails(b, i)
                    if i == 2:
                        projection_tail(b, VA)
                    if i in (4, 7) and not last:
                        projection_tail(b + 1, {4: K0, 7: Q1}[i])
                    if i + 2 < BLOCKS or not last:
                        inverse_sum(*ahead)
                    if first and i == 0:
                        channel_spreads(1, BATCHES, 2, mixed)
                    if first and i == 1:
                        variances(1, BATCHES, 2, mixed)
                    if first and i == 2:
                        coefficients(1, BATCHES, 2, mixed)
                    if i == 2:
                        normalised(b + 1, (b + 1) % BATCHES)
                    if i == 3 and not first:
                        results(b - 1, 1)
                    if i == 7:
                        results(b, 0)

            steps(0, 0, QB, first=True)
            with dve.Fori(0, BATCHES - 1) as b:
                steps(b, QB, BLOCKS)
                steps(b + 1, 0, QB)
            steps(BATCHES - 1, QB, BLOCKS, last=True)
            results(BATCHES - 1, 1, projected)

        @block_ctx.tensor
        def _(pe):
            def group_means(lo, hi, sums):
                pe.wait_ge(s_means, hi)
                pe.matmul(sums[:, lo:hi], group_mean[:, :], mean_var[:, lo:hi, 0],
                          start=True, stop=True).then_inc(s_gmean, 1)

            def group_variances(lo, hi, n, sums):
                pe.wait_ge(s_spread, n)
                pe.matmul(sums[:, 8 + lo:8 + hi], group_mean[:, :], spread[:, lo:hi],
                          start=True, stop=True).then_inc(s_gvar, 1)

            def split_product(to, w_hi, w_lo, m_hi, m_lo):
                pe.matmul(to, w_hi, m_hi, start=True, stop=False)
                pe.matmul(to, w_hi, m_lo, start=False, stop=False)
                return pe.matmul(to, w_lo, m_hi, start=False, stop=True)

            def projection(c, p, bank=projected):
                if bank is projected:
                    wait(pe, s_pj_lo, PJ * c + p)
                if p == K0 and not isinstance(c, int):
                    pe.wait_ge(s_y_lo, c)
                if p in (K0, K1, Q0, Q1):
                    h = (p - K0) % 2
                    w_hi, w_lo = (wk_hi, wk_lo) if p in (K0, K1) else (wq_hi, wq_lo)
                    half = slice(h * HALF, (h + 1) * HALF)
                    mm = split_product(bank[:, 0:HALF], w_hi[:, :], w_lo[:, :], y_hi[:, half], y_lo[:, half])
                else:
                    if p == VA:
                        pe.wait_ge(s_y_keys, c + 1)
                    for j in range(KB):
                        key = ((p - VA) * KB + j) * 128
                        mm = pe.matmul(projected[:, j * 128:(j + 1) * 128], y_keys[:, key:key + 128],
                                       wv_out[:, :], start=True, stop=True)
                mm.then_inc(s_pj, 1)

            def block_scores(b, i):
                if i == 0:
                    pe.wait_ge(s_pj_lo, PJ * b + Q0 + 1)
                if i == QB:
                    pe.wait_ge(s_pj_lo, PJ * b + Q1 + 1)
                wait(pe, s_exp, BLOCKS * b + i - 1)
                query = slice(i * 128, (i + 1) * 128)
                keys = [bass.ds(b % 2 * N + h * HALF, HALF) for h in range(HALVES)]
                to = [scores[:, i % 2, h * HALF:(h + 1) * HALF] for h in range(HALVES)]
                for h in range(HALVES):
                    pe.matmul(to[h], q_hi[:, query], k_hi[:, keys[h]], start=True, stop=False)
                    pe.matmul(to[h], q_hi[:, query], k_lo[:, keys[h]], start=False, stop=False)
                for h in range(HALVES):
                    mm = pe.matmul(to[h], q_lo[:, query], k_hi[:, keys[h]], start=False, stop=True)
                mm.then_inc(s_scores, 1)

            def turn(b, i):
                pe.wait_ge(s_probs, BLOCKS * b + i + 1)
                for j in range(2):
                    wait(pe, s_pt_lo, 2 * (BLOCKS * b + i - 1) + j + 1)
                    for k in range(KB):
                        key = (j * KB + k) * 128
                        mm = pe.transpose(turned[:, j, k * 128:(k + 1) * 128],
                                          probs[:, i % RING, key:key + 128], ident[:, :])
                    mm.then_inc(s_turned, 1)

            def mix(b, g, chunk, bank=mixed):
                group = PAIR_GROUPS * b + g
                if chunk == 0 and bank is mixed:
                    wait(pe, s_result, group)
                if chunk % 2 == 0:
                    pe.wait_ge(s_pt_lo, 2 * (QB * group + QB - 1) + chunk // 2 + 1)
                    if g == 0:
                        pe.wait_ge(s_pj_lo, PJ * b + (VA, VB)[chunk // 2] + 1)
                for k in range(PAIR * chunk, PAIR * (chunk + 1)):
                    channels = slice(k * 128, (k + 1) * 128)
                    pe.matmul(bank[:, :], v_hi[:, channels], pt_hi[:, g, k, :], start=(k == 0), stop=False)
                    pe.matmul(bank[:, :], v_hi[:, channels], pt_lo[:, g, k, :], start=False, stop=False)
                    mm = pe.matmul(bank[:, :], v_lo[:, channels], pt_hi[:, g, k, :], start=False,
                                   stop=(k == BLOCKS - 1))
                mm.then_inc(s_mixed, 1)

            pe.wait_ge(s_const, 4 + GROUPS)
            group_means(0, 1, projected)
            group_variances(0, 1, 1, projected)
            pe.wait_ge(s_w, 16)
            pe.wait_ge(s_vecs, 16)
            pe.matmul(scores[:, 1, 0:C], WV, WOUT_T, start=True, stop=True)
            pe.matmul(scores[:, 1, C:C + 1], WOUT_T, BV, start=True, stop=True).then_inc(s_wv, 1)
            for _ in range(WARM):
                pe.transpose(scores[:, 0, 0:128], ident[:, :], ident[:, :])
            pe.wait_ge(s_norm, 1)
            pe.wait_ge(s_w_lo, 2)
            pe.wait_ge(s_y_lo_first, 1)
            projection(0, K0, FIRST_BANK[K0])
            pe.wait_ge(s_y_lo_first, 2)
            for p in (K1, Q0, Q1):
                projection(0, p, FIRST_BANK[p])
            block_scores(0, 0)
            pe.wait_ge(s_wv_out, 2)
            block_scores(0, 1)

            def steps(b, lo, hi, last=False, first=False):
                for i in range(lo, hi):
                    scored = (b, i + 2) if i + 2 < BLOCKS else (b + 1, i + 2 - BLOCKS)
                    ahead = i + 2 < BLOCKS or not last
                    if i == 6 and not last:
                        projection(b + 1, Q0)
                    elif ahead:
                        block_scores(*scored)
                    if i == 5 and not last:
                        projection(b + 1, K1)
                    turn(b, i)
                    if first and i == 0:
                        group_means(1, BATCHES, mixed)
                    if first and i == 1:
                        group_variances(1, BATCHES, 2, mixed)
                    if i == 2:
                        projection(b, VA)
                    if i in (4, 7) and not last:
                        projection(b + 1, {4: K0, 7: Q1}[i])
                    if i >= QB:
                        mix(b, 0, i - QB)
                    elif not first:
                        mix(b - 1, 1, i)
                    if i == 6 and ahead:
                        block_scores(*scored)
                    if i == 3:
                        projection(b, VB)

            steps(0, 0, QB, first=True)
            with pe.Fori(0, BATCHES - 1) as b:
                steps(b, QB, BLOCKS)
                steps(b + 1, 0, QB)
            steps(BATCHES - 1, QB, BLOCKS, last=True)
            for chunk in range(QB):
                mix(BATCHES - 1, 1, chunk, projected)


WARM = 12
PAIR_GROUPS = 2


_N = 'L0_conv_'


def kernel(**inputs):
    import numpy as _np
    import concourse.bacc as _bacc
    from concourse import mybir as _mybir
    from concourse.bass_utils import run_bass_kernel_spmd as _run

    x = _np.ascontiguousarray(inputs['x'])
    c = x.shape[1]
    wq, wk, wv = _np.asarray(inputs[_N + 'w_qkv']).reshape(3, c, c)
    bq, bk, bv = _np.asarray(inputs[_N + 'b_qkv']).reshape(3, c)
    vectors = _np.ascontiguousarray(_np.stack(
        [inputs[_N + 'gn_gamma'], inputs[_N + 'gn_beta'], bq, bk, bv, inputs[_N + 'b_out']], axis=1))
    weights = _np.ascontiguousarray(_np.concatenate(
        [wq.T, wk.T, wv, _np.asarray(inputs[_N + 'w_out']).T], axis=1))

    nc = _bacc.Bacc("TRN2", target_bir_lowering=False, num_devices=1)
    arrays, args = {}, []
    for name, a in (("x", x), ("vectors", vectors), ("weights", weights)):
        arrays[f"in_{name}_dram"] = a
        args.append(nc.dram_tensor(f"in_{name}_dram", a.shape, _mybir.dt.from_np(a.dtype), kind="ExternalInput").ap())
    args.append(nc.dram_tensor("out_0_dram", x.shape, _mybir.dt.float32, kind="ExternalOutput").ap())
    attention_kernel(nc, *args)
    r = _run(nc, [arrays], core_ids=[0])
    return r.results[0]["out_0_dram"]
```

```python
import concourse.bass as bass
from concourse import mybir
from contextlib import ExitStack


def attention_kernel(nc, x, vectors, weights, out):
    fp32 = mybir.dt.float32
    fp32r = mybir.dt.float32r
    ALU = mybir.AluOpType
    ACT = mybir.ActivationFunctionType
    AX = mybir.AxisListType

    BATCHES, C, H, W = x.shape
    N = H * W
    GROUPS = 4
    CG = C // GROUPS
    EPS = 1e-5
    SCALE = float(C) ** -0.5
    HALF = 512
    HALVES = N // HALF
    BLOCKS = N // 128
    QB = HALF // 128
    KB = HALF // 128
    PAIR = BLOCKS // QB
    PJ = 6
    K0, Q0, K1, Q1, VA, VB = range(PJ)
    RING = 4

    x_v = x.rearrange("b c h w -> b c (h w)")
    out_v = out.rearrange("b c h w -> b c (h w)")

    ctx = ExitStack()
    with ctx:
        def sb(name, shape, dt=fp32):
            return ctx.enter_context(nc.sbuf_tensor(name, shape, dt))

        def ps(name, shape):
            return ctx.enter_context(nc.psum_tensor(name, shape, fp32))

        def sem(name):
            return ctx.enter_context(nc.semaphore(name))

        xs = sb("xs", [C, BATCHES * N])
        vecs = sb("vecs", [C, 6])
        GAMMA, BETA, BQ, BK, BV, BOUT = (vecs[:, i:i + 1] for i in range(6))
        ws = sb("ws", [128, 4, C])
        WQ_T, WK_T, WV, WOUT_T = (ws[:, i, :] for i in range(4))
        blank = sb("blank", [128, 128])
        ident = sb("ident", [128, 128])
        group_mean = sb("group_mean", [128, 128])
        minus_mean = sb("minus_mean", [128, 128])
        minus_half = sb("minus_half", [128, BATCHES])
        centring = sb("centring", [128, 128])
        wq_hi, wq_lo = sb("wq_hi", [C, C], fp32r), sb("wq_lo", [C, C], fp32r)
        wk_hi, wk_lo = sb("wk_hi", [C, C], fp32r), sb("wk_lo", [C, C], fp32r)
        wv_out = sb("wv_out", [C, C])
        bq_scaled = sb("bq_scaled", [C, 1])
        out_bias = sb("out_bias", [C, 1])
        stats = sb("stats", [C, BATCHES * HALVES, 6])
        mean_var = sb("mean_var", [C, BATCHES, 2])
        spread = sb("spread", [C, BATCHES])
        var_eps = sb("var_eps", [C, BATCHES])
        rstd = sb("rstd", [C, BATCHES])
        norm_a = sb("norm_a", [C, BATCHES])
        norm_b = sb("norm_b", [C, BATCHES])
        y = sb("y", [C, N])
        y_hi, y_lo = sb("y_hi", [C, N], fp32r), sb("y_lo", [C, N], fp32r)
        y_keys = sb("y_keys", [C, N])
        q_hi, q_lo = sb("q_hi", [C, N], fp32r), sb("q_lo", [C, N], fp32r)
        k_hi, k_lo = sb("k_hi", [C, 2 * N], fp32r), sb("k_lo", [C, 2 * N], fp32r)
        v_hi, v_lo = sb("v_hi", [128, N], fp32r), sb("v_lo", [128, N], fp32r)
        neg_max = sb("neg_max", [128, BLOCKS])
        row_sum = sb("row_sum", [128, BLOCKS])
        inv_sum = sb("inv_sum", [128, BLOCKS])
        probs = sb("probs", [128, RING, N])
        pt_hi = sb("pt_hi", [128, 2, BLOCKS, HALF], fp32r)
        pt_lo = sb("pt_lo", [128, 2, BLOCKS, HALF], fp32r)
        result = sb("result", [C, 2, HALF])
        whole = {Q1: result[:, 0, :], VA: result[:, 1, :]}

        scores = ps("scores", [128, 2, N])
        turned = ps("turned", [128, 2, HALF])
        mixed = ps("mixed", [C, HALF])
        projected = ps("projected", [128, HALF])
        FIRST_BANK = (projected, mixed, turned[:, 0, :], turned[:, 1, :])
        DEV, MINUS_MEAN, VARIANCE = 0, 8, 16

        s_x = [sem(f"x_loaded{b}") for b in range(BATCHES)]
        s_x0_right = sem("right_half_of_first_x_loaded")
        s_x1_right = sem("right_half_of_second_x_loaded")
        s_w = sem("weights_loaded")
        s_vecs = sem("vectors_loaded")
        s_blank = sem("blank_made")
        s_const = sem("constants_made")
        s_step = sem("dve_step")
        s_means = sem("channel_means_ready")
        s_gmean = sem("group_means_ready")
        s_spread = sem("channel_spreads_ready")
        s_gvar = sem("group_variances_ready")
        s_var_eps = sem("variance_eps_ready")
        s_rstd = sem("rstd_ready")
        s_norm = sem("norm_ready")
        s_w_hi = sem("weight_heads_ready")
        s_w_lo = sem("weight_tails_ready")
        s_wv = sem("folded_weights_ready")
        s_wv_out = sem("folded_weights_taken")
        s_y = sem("y_ready")
        s_y_0a = sem("first_y_left_half_ready")
        s_y_0b = sem("first_y_right_half_ready")
        s_y_hi_0 = sem("first_y_head_half_ready")
        s_y_lo_0a = sem("first_y_tail_left_half_ready")
        s_y_lo_0b = sem("first_y_tail_right_half_ready")
        s_y_hi = sem("y_head_ready")
        s_y_lo = sem("y_tail_ready")
        s_y_keys = sem("y_keys_ready")
        s_pj = sem("projected_ready")
        s_pj_hi = sem("projection_head_ready")
        s_pj_lo = sem("projection_tail_ready")
        s_whole = sem("whole_projection_copied")
        s_scores = sem("scores_ready")
        s_max = sem("max_ready")
        s_exp = sem("exp_ready")
        s_inv = sem("inv_sum_ready")
        s_probs = sem("probs_normalised")
        s_turned = sem("probs_turned")
        s_pt_hi = sem("turned_head_ready")
        s_pt_lo = sem("turned_tail_ready")
        s_mixed = sem("mixed_chunk_done")
        s_result = sem("result_ready")
        s_stored = [sem("stored_even"), sem("stored_odd")]
        s_pool = sem("pool_go")

        block_ctx = ctx.enter_context(nc.Block())

        def wait(eng, s, value):
            if isinstance(value, int) and value <= 0:
                return
            eng.wait_ge(s, value)

        @block_ctx.sync
        def _(sp):
            sp.dma_start(xs[:, 0:HALF], x_v[0, :, 0:HALF]).then_inc(s_x[0], 16)
            sp.dma_start(ws[:, :, :], weights.rearrange("p (t c) -> p t c", t=4)).then_inc(s_w, 16)
            for h in range(HALVES):
                half = slice(h * HALF, (h + 1) * HALF)
                sp.dma_start(xs[:, N + h * HALF:N + (h + 1) * HALF],
                             x_v[1, :, half]).then_inc((s_x[1], s_x1_right)[h], 16)
            for b in range(2, BATCHES):
                sp.dma_start(xs[:, b * N:(b + 1) * N], x_v[b]).then_inc(s_x[b], 16)

            def store(b, g):
                sp.wait_ge(s_result, PAIR_GROUPS * b + g + 1)
                sp.dma_start(out_v[b, :, g * HALF:(g + 1) * HALF] if isinstance(b, int) else
                             out_v[bass.ds(b, 1), :, g * HALF:(g + 1) * HALF].rearrange("b c n -> (b c) n"),
                             result[:, g, :]).then_inc(s_stored[g], 16)

            with sp.Fori(0, BATCHES) as b:
                for g in range(PAIR_GROUPS):
                    store(b, g)
            for g in range(PAIR_GROUPS):
                sp.wait_ge(s_stored[g], 16 * BATCHES)

        @block_ctx.gpsimd
        def _(pool):
            pool.memset(ident[:, :], 0.0).then_inc(s_const, 1)
            pool.memset(group_mean[:, :], 0.0).then_inc(s_const, 1)
            pool.memset(minus_half[:, :], -0.5).then_inc(s_const, 1)
            pool.wait_ge(s_const, 3)
            pool.affine_select(out=ident[:, :], in_=ident[:, :], compare_op=ALU.not_equal, fill=1.0,
                               base=0, pattern=[[-1, 128]], channel_multiplier=1).then_inc(s_const, 1)
            for g in range(GROUPS):
                pool.wait_ge(s_const, 4 + g)
                pool.memset(group_mean[g * CG:(g + 1) * CG, g * CG:(g + 1) * CG], 1.0 / CG).then_inc(s_const, 1)
            pool.wait_ge(s_const, 4 + GROUPS)
            pool.tensor_tensor(centring[:, :], ident[:, :], group_mean[:, :], ALU.subtract).then_inc(s_const, 1)
            pool.tensor_scalar(minus_mean[:, :], group_mean[:, :], -1.0, None, ALU.mult).then_inc(s_const, 1)

            def rstd_of(lo, hi, n):
                pool.wait_ge(s_var_eps, n)
                pool.tensor_tensor(rstd[:, lo:hi], var_eps[:, lo:hi], minus_half[:, lo:hi],
                                   ALU.pow).then_inc(s_rstd, 1)

            def normalised_second():
                pool.wait_ge(s_norm, 2)
                pool.wait_ge(s_y_lo_0a, 1)
                pool.wait_ge(s_y_lo_0b, 1)
                pool.wait_ge(s_y_keys, 1)
                pool.tensor_scalar(y[:, :], xs[:, N:2 * N], norm_a[:, 1:2], norm_b[:, 1:2],
                                   ALU.mult, ALU.add).then_inc(s_y, 1)

            def y_tail(c, h):
                half = slice(h * HALF, (h + 1) * HALF)
                pool.wait_ge(s_y, c)
                pool.wait_ge(s_y_hi, c)
                pool.tensor_tensor(y_lo[:, half], y[:, half], y_hi[:, half].bitcast(fp32),
                                   ALU.subtract).then_inc(s_y_lo, 1)

            def first_tail(p, head, tail):
                half = slice(HALF, N) if p == Q1 else slice(0, HALF)
                pool.wait_ge(s_pj_lo, p)
                pool.wait_ge(s_pj_hi, p + 1)
                pool.wait_ge(s_whole, (Q1, VA).index(p) + 1)
                pool.tensor_tensor(tail[:, half], whole[p], head[:, half].bitcast(fp32),
                                   ALU.subtract).then_inc(s_pj_lo, 1)

            def normalise(b, i):
                pool.wait_ge(s_inv, BLOCKS * b + i + 1)
                pool.sem_inc(s_pool, 1)
                pool.tensor_scalar(probs[:, i % RING, :], probs[:, i % RING, :], inv_sum[:, i:i + 1], 1.0,
                                   ALU.mult, ALU.mult).then_inc(s_probs, 1)

            rstd_of(0, 1, 1)
            right = slice(HALF, N)
            pool.wait_ge(s_norm, 1)
            pool.tensor_scalar(y[:, right], xs[:, right], norm_a[:, 0:1], norm_b[:, 0:1],
                               ALU.mult, ALU.add).then_inc(s_y_0b, 1)
            pool.wait_ge(s_y_0b, 1)
            pool.wait_ge(s_y_hi_0, 2)
            pool.tensor_tensor(y_lo[:, right], y[:, right], y_hi[:, right].bitcast(fp32),
                               ALU.subtract).then_inc(s_y_lo_0b, 1)
            first_tail(Q1, q_hi, q_lo)
            rstd_of(1, 2, 2)
            normalise(0, 0)
            normalise(0, 1)
            normalised_second()
            first_tail(VA, v_hi, v_lo)

            def steps(b, lo, hi, last=False, first=False):
                for i in range(lo, hi):
                    if i == 3 and not first:
                        y_tail(b + 1, 0)
                    if i + 2 < BLOCKS:
                        normalise(b, i + 2)
                    elif not last:
                        normalise(b + 1, i + 2 - BLOCKS)
                    if first and i == 1:
                        y_tail(1, 0)
                        y_tail(1, 1)
                    if first and i == 2:
                        rstd_of(2, BATCHES, 3)
                    if not first and i == 3:
                        y_tail(b + 1, 1)

            steps(0, 0, QB, first=True)
            with pool.Fori(0, BATCHES - 1) as b:
                steps(b, QB, BLOCKS)
                steps(b + 1, 0, QB)
            steps(BATCHES - 1, QB, BLOCKS, last=True)

        @block_ctx.scalar
        def _(act):
            act.dma_start(xs[:, HALF:N], x_v[0, :, HALF:N]).then_inc(s_x0_right, 16)
            act.dma_start(vecs[:, :], vectors).then_inc(s_vecs, 16)

            def y_head(c):
                act.wait_ge(s_y, c)
                act.wait_ge(s_pj, PJ * c - PJ + Q1 + 1)
                act.activation(y_hi[:, :], y[:, :], ACT.Copy).then_inc(s_y_hi, 1)

            def keep_y(c):
                if isinstance(c, int):
                    act.wait_ge(s_y_0a, 1)
                    act.wait_ge(s_y_0b, 1)
                else:
                    act.wait_ge(s_y, c)
                if not isinstance(c, int) or c >= 1:
                    act.wait_ge(s_pj, PJ * c)
                act.activation(y_keys[:, :], y[:, :], ACT.Copy).then_inc(s_y_keys, 1)

            def projection_head(c, p, bank=projected):
                act.wait_ge(s_pj, PJ * c + p + 1)
                bank = bank[:, 0:HALF]
                if p in (K0, K1):
                    half = bass.ds(c % 2 * N + (p - K0) // 2 * HALF, HALF)
                    act.activation(k_hi[:, half], bank, ACT.Identity, bias=BK).then_inc(s_pj_hi, 1)
                elif p in (Q0, Q1):
                    half = bass.ds((p - Q0) // 2 * HALF, HALF)
                    act.activation(q_hi[:, half], bank, ACT.Identity,
                                   bias=bq_scaled[:, :]).then_inc(s_pj_hi, 1)
                else:
                    half = bass.ds((p - VA) * HALF, HALF)
                    act.activation(v_hi[:, half], bank, ACT.Copy).then_inc(s_pj_hi, 1)

            def whole_copy(p, bank):
                act.activation(whole[p], bank[:, 0:HALF], ACT.Identity,
                               bias=bq_scaled[:, :] if p == Q1 else 0.0).then_inc(s_whole, 1)

            def exponentials(b, i):
                act.wait_ge(s_max, BLOCKS * b + i + 1)
                wait(act, s_turned, 2 * (BLOCKS * b + i - RING + 1))
                act.activation(probs[:, i % RING, :], scores[:, i % 2, :], ACT.Exp,
                               bias=neg_max[:, i:i + 1], accum_out=row_sum[:, i:i + 1]).then_inc(s_exp, 1)

            def turned_heads(b, i):
                g = i // QB
                if i % QB == 0:
                    wait(act, s_mixed, QB * (PAIR_GROUPS * b + g - 1))
                for j in range(2):
                    act.wait_ge(s_turned, 2 * (BLOCKS * b + i) + j + 1)
                    act.activation(pt_hi[:, g, j * KB:(j + 1) * KB, i % QB * 128:(i % QB + 1) * 128],
                                   turned[:, j, :].rearrange("p (k n) -> p k n", k=KB),
                                   ACT.Copy).then_inc(s_pt_hi, 1)

            act.wait_ge(s_w, 16)
            act.activation(wq_hi[:, :], WQ_T, ACT.Copy, scale=SCALE).then_inc(s_w_hi, 1)
            act.activation(wk_hi[:, :], WK_T, ACT.Copy).then_inc(s_w_hi, 1)
            act.wait_ge(s_norm, 1)
            for h in range(HALVES):
                half = slice(h * HALF, (h + 1) * HALF)
                act.activation(y_hi[:, half], xs[:, half], ACT.Identity, scale=norm_a[:, 0:1],
                               bias=norm_b[:, 0:1]).then_inc(s_y_hi_0, 1)
            act.wait_ge(s_w_lo, 3)
            for p in (K0, Q0, K1, Q1):
                projection_head(0, p, FIRST_BANK[p])
            whole_copy(Q1, FIRST_BANK[Q1])
            keep_y(0)
            exponentials(0, 0)
            exponentials(0, 1)
            projection_head(0, VA)
            whole_copy(VA, projected)

            def steps(b, lo, hi, last=False, first=False):
                for i in range(lo, hi):
                    if i in (5, 6) and not last:
                        projection_head(b + 1, {5: Q0, 6: K1}[i])
                    turned_heads(b, i)
                    if i == 2 and not first:
                        projection_head(b, VA)
                    if first and i == 3:
                        projection_head(b, VB)
                    if i in (4, 7) and not last:
                        projection_head(b + 1, {4: K0, 7: Q1}[i])
                    if i + 2 < BLOCKS:
                        exponentials(b, i + 2)
                    elif not last:
                        exponentials(b + 1, i + 2 - BLOCKS)
                    if i == (1 if first else 2):
                        y_head(b + 1)
                    if i == 3 and not first:
                        projection_head(b, VB)
                    if i == 4 and not last:
                        keep_y(b + 1)

            steps(0, 0, QB, first=True)
            with act.Fori(0, BATCHES - 1) as b:
                steps(b, QB, BLOCKS)
                steps(b + 1, 0, QB)
            steps(BATCHES - 1, QB, BLOCKS, last=True)

        @block_ctx.vector
        def _(dve):
            steps_done = [0]

            def step(ins):
                steps_done[0] += 1
                ins.then_inc(s_step, 1)

            def own_steps():
                dve.wait_ge(s_step, steps_done[0])

            def half_stats(b, h):
                if b > 1:
                    dve.wait_ge(s_x[b], 16)
                else:
                    dve.wait_ge((s_x[b], (s_x0_right, s_x1_right)[b])[h], 16)
                step(dve.bn_stats(stats[:, b * HALVES + h, :],
                                  xs[:, b * N + h * HALF:b * N + (h + 1) * HALF]))

            def channel_stats(lo, hi):
                own_steps()
                for b in range(lo, hi):
                    mm = dve.bn_aggr(mean_var[:, b, :], stats[:, b * HALVES:(b + 1) * HALVES, :]
                                     .rearrange("p a k -> p (a k)"))
                    mm.then_inc(s_means, 1)

            def channel_spreads(lo, hi, matmuls, sums):
                dve.wait_ge(s_gmean, matmuls)
                for b in range(lo, hi):
                    deviation = sums[:, DEV + b:DEV + b + 1]
                    mm = dve.scalar_tensor_tensor(out=spread[:, b:b + 1], in0=deviation, scalar=deviation,
                                                  in1=mean_var[:, b, 1:2], op0=ALU.mult, op1=ALU.add)
                    mm.then_inc(s_spread, 1)

            def variances(lo, hi, n, sums):
                dve.wait_ge(s_gvar, n)
                dve.tensor_scalar(var_eps[:, lo:hi], sums[:, VARIANCE + lo:VARIANCE + hi], EPS, None,
                                  ALU.add).then_inc(s_var_eps, 1)

            def coefficients(lo, hi, n, minus_means):
                dve.wait_ge(s_rstd, n)
                dve.wait_ge(s_gmean, 2 * n)
                step(dve.tensor_scalar(norm_a[:, lo:hi], rstd[:, lo:hi], GAMMA, None, ALU.mult))
                own_steps()
                for b in range(lo, hi):
                    mm = dve.scalar_tensor_tensor(out=norm_b[:, b:b + 1], in0=minus_means[:, MINUS_MEAN + b:MINUS_MEAN + b + 1], scalar=norm_a[:, b:b + 1],
                                                  in1=BETA, op0=ALU.mult, op1=ALU.add)
                    if b == hi - 1:
                        mm.then_inc(s_norm, 1)
                    else:
                        step(mm)

            def normalised(c, source):
                dve.wait_ge(s_y_lo, HALVES * (c - 1))
                dve.wait_ge(s_y_keys, c)
                dve.tensor_scalar(y[:, :], xs[:, bass.ds(source * N, N)], norm_a[:, bass.ds(source, 1)],
                                  norm_b[:, bass.ds(source, 1)], ALU.mult, ALU.add).then_inc(s_y, 1)

            def projection_tail(c, p, bank=projected):
                dve.wait_ge(s_pj_hi, PJ * c + p + 1)
                bank = bank[:, 0:HALF]
                if p in (K0, K1):
                    half = bass.ds(c % 2 * N + (p - K0) // 2 * HALF, HALF)
                    dve.scalar_tensor_tensor(out=k_lo[:, half], in0=bank, scalar=BK,
                                             in1=k_hi[:, half].bitcast(fp32), op0=ALU.add,
                                             op1=ALU.subtract).then_inc(s_pj_lo, 1)
                elif p in (Q0, Q1):
                    half = bass.ds((p - Q0) // 2 * HALF, HALF)
                    dve.scalar_tensor_tensor(out=q_lo[:, half], in0=bank, scalar=bq_scaled[:, :],
                                             in1=q_hi[:, half].bitcast(fp32), op0=ALU.add,
                                             op1=ALU.subtract).then_inc(s_pj_lo, 1)
                else:
                    half = bass.ds((p - VA) * HALF, HALF)
                    dve.tensor_tensor(v_lo[:, half], bank, v_hi[:, half].bitcast(fp32),
                                      ALU.subtract).then_inc(s_pj_lo, 1)

            def maximum(b, i):
                dve.wait_ge(s_scores, BLOCKS * b + i + 1)
                dve.tensor_reduce(neg_max[:, i:i + 1], scores[:, i % 2, :], AX.X, ALU.max,
                                  negate=True).then_inc(s_max, 1)

            def inverse_sum(b, i):
                dve.wait_ge(s_exp, BLOCKS * b + i + 1)
                dve.reciprocal(inv_sum[:, i:i + 1], row_sum[:, i:i + 1]).then_inc(s_inv, 1)

            def turned_tails(b, i):
                g = i // QB
                for j in range(2):
                    dve.wait_ge(s_pt_hi, 2 * (BLOCKS * b + i) + j + 1)
                    at = (slice(None), g, slice(j * KB, (j + 1) * KB), slice(i % QB * 128, (i % QB + 1) * 128))
                    dve.tensor_tensor(pt_lo[at], turned[:, j, :].rearrange("p (k n) -> p k n", k=KB),
                                      pt_hi[at].bitcast(fp32), ALU.subtract).then_inc(s_pt_lo, 1)

            def results(b, g, bank=mixed):
                group = PAIR_GROUPS * b + g
                dve.wait_ge(s_mixed, QB * (group + 1))
                if not isinstance(b, int) or b >= 1:
                    dve.wait_ge(s_stored[g], 16 * b)
                dve.scalar_tensor_tensor(out=result[:, g, :], in0=bank[:, :], scalar=out_bias[:, :],
                                         in1=xs[:, bass.ds(b * N + g * HALF, HALF)], op0=ALU.add,
                                         op1=ALU.add).then_inc(s_result, 1)

            dve.memset(blank[:, :], 0.0).then_inc(s_blank, 1)
            half_stats(0, 0)
            half_stats(0, 1)
            channel_stats(0, 1)
            channel_spreads(0, 1, 1, projected)
            dve.wait_ge(s_w_hi, 1)
            dve.scalar_tensor_tensor(out=wq_lo[:, :], in0=WQ_T, scalar=SCALE,
                                     in1=wq_hi[:, :].bitcast(fp32), op0=ALU.mult,
                                     op1=ALU.subtract).then_inc(s_w_lo, 1)
            half_stats(1, 0)
            variances(0, 1, 1, projected)
            dve.wait_ge(s_w_hi, 2)
            dve.tensor_tensor(wk_lo[:, :], WK_T, wk_hi[:, :].bitcast(fp32),
                              ALU.subtract).then_inc(s_w_lo, 1)
            half_stats(1, 1)
            dve.wait_ge(s_vecs, 16)
            coefficients(0, 1, 1, mixed)
            left = slice(0, HALF)
            dve.wait_ge(s_norm, 1)
            dve.tensor_scalar(y[:, left], xs[:, left], norm_a[:, 0:1], norm_b[:, 0:1],
                              ALU.mult, ALU.add).then_inc(s_y_0a, 1)
            dve.tensor_scalar(bq_scaled[:, :], BQ, SCALE, None, ALU.mult).then_inc(s_w_lo, 1)
            dve.wait_ge(s_y_0a, 1)
            dve.wait_ge(s_y_hi_0, 1)
            dve.tensor_tensor(y_lo[:, left], y[:, left], y_hi[:, left].bitcast(fp32),
                              ALU.subtract).then_inc(s_y_lo_0a, 1)
            dve.wait_ge(s_wv, 1)
            dve.tensor_copy(wv_out[:, :], scores[:, 1, 0:C]).then_inc(s_wv_out, 1)
            dve.tensor_tensor(out_bias[:, :], scores[:, 1, C:C + 1], BOUT, ALU.add).then_inc(s_wv_out, 1)
            channel_stats(1, 2)
            half_stats(2, 0)
            half_stats(2, 1)
            projection_tail(0, K0, FIRST_BANK[K0])
            projection_tail(0, Q0, FIRST_BANK[Q0])
            projection_tail(0, K1, FIRST_BANK[K1])
            half_stats(3, 0)
            channel_spreads(1, 2, 4, mixed)
            maximum(0, 0)
            maximum(0, 1)
            variances(1, 2, 2, mixed)
            inverse_sum(0, 0)
            half_stats(3, 1)
            inverse_sum(0, 1)
            channel_stats(2, BATCHES)
            coefficients(1, 2, 2, mixed)

            def steps(b, lo, hi, last=False, first=False):
                for i in range(lo, hi):
                    ahead = (b, i + 2) if i + 2 < BLOCKS else (b + 1, i + 2 - BLOCKS)
                    if i == 6 and not last:
                        projection_tail(b + 1, K1)
                        turned_tails(b, i)
                    if i + 2 < BLOCKS or not last:
                        maximum(*ahead)
                    if i == 5 and not last:
                        projection_tail(b + 1, Q0)
                    if i != 6 or last:
                        turned_tails(b, i)
                    if i == 2 and not first:
                        projection_tail(b, VA)
                    if i == 4 and not last:
                        projection_tail(b + 1, K0)
                    if i == 7:
                        results(b, 0)
                    if i == 3 and not first:
                        results(b - 1, 1)
                    if i == 3 and first:
                        projection_tail(b, VB)
                    if i + 2 < BLOCKS or not last:
                        inverse_sum(*ahead)
                    if i == 7 and not last:
                        projection_tail(b + 1, Q1)
                    if first and i == 1:
                        channel_spreads(2, BATCHES, 6, mixed)
                    if first and i == 2:
                        variances(2, BATCHES, 3, mixed)
                    if first and i == 3:
                        coefficients(2, BATCHES, 3, mixed)
                    if i == 2 and not first:
                        normalised(b + 1, (b + 1) % BATCHES)
                    if i == 3 and not first:
                        projection_tail(b, VB)

            steps(0, 0, QB, first=True)
            with dve.Fori(0, BATCHES - 1) as b:
                steps(b, QB, BLOCKS)
                steps(b + 1, 0, QB)
            steps(BATCHES - 1, QB, BLOCKS, last=True)
            results(BATCHES - 1, 1, projected)

        @block_ctx.tensor
        def _(pe):
            def minus_group_means(lo, hi, minus_means):
                pe.matmul(minus_means[:, MINUS_MEAN + lo:MINUS_MEAN + hi], minus_mean[:, :],
                          mean_var[:, lo:hi, 0], start=True, stop=True).then_inc(s_gmean, 1)

            def group_means(lo, hi, sums, minus_means=None):
                pe.wait_ge(s_means, hi)
                pe.matmul(sums[:, DEV + lo:DEV + hi], centring[:, :], mean_var[:, lo:hi, 0],
                          start=True, stop=True).then_inc(s_gmean, 1)
                if minus_means is not None:
                    minus_group_means(lo, hi, minus_means)

            def group_variances(lo, hi, sums):
                pe.wait_ge(s_spread, hi)
                pe.matmul(sums[:, VARIANCE + lo:VARIANCE + hi], group_mean[:, :], spread[:, lo:hi],
                          start=True, stop=True).then_inc(s_gvar, 1)

            def split_product(to, w_hi, w_lo, m_hi, m_lo):
                pe.matmul(to, w_hi, m_hi, start=True, stop=False)
                pe.matmul(to, w_hi, m_lo, start=False, stop=False)
                return pe.matmul(to, w_lo, m_hi, start=False, stop=True)

            def projection(c, p, bank=projected):
                if bank is projected:
                    wait(pe, s_pj_lo, PJ * c + p)
                if p in (K0, K1):
                    pe.wait_ge(s_y_lo, HALVES * (c - 1) + p // 2 + 1)
                if p in (K0, K1, Q0, Q1):
                    h = p // 2
                    w_hi, w_lo = (wk_hi, wk_lo) if p in (K0, K1) else (wq_hi, wq_lo)
                    half = slice(h * HALF, (h + 1) * HALF)
                    mm = split_product(bank[:, 0:HALF], w_hi[:, :], w_lo[:, :], y_hi[:, half], y_lo[:, half])
                else:
                    if p == VA:
                        pe.wait_ge(s_y_keys, c + 1)
                    for j in range(KB):
                        key = ((p - VA) * KB + j) * 128
                        mm = pe.matmul(projected[:, j * 128:(j + 1) * 128], y_keys[:, key:key + 128],
                                       wv_out[:, :], start=True, stop=True)
                mm.then_inc(s_pj, 1)

            def block_scores(b, i):
                if i == 0:
                    pe.wait_ge(s_pj_lo, PJ * b + K1 + 1)
                if i == QB:
                    pe.wait_ge(s_pj_lo, PJ * b + Q1 + 1)
                wait(pe, s_exp, BLOCKS * b + i - 1)
                query = slice(i * 128, (i + 1) * 128)
                keys = [bass.ds(b % 2 * N + h * HALF, HALF) for h in range(HALVES)]
                to = [scores[:, i % 2, h * HALF:(h + 1) * HALF] for h in range(HALVES)]
                for h in range(HALVES):
                    pe.matmul(to[h], q_hi[:, query], k_hi[:, keys[h]], start=True, stop=False)
                    pe.matmul(to[h], q_hi[:, query], k_lo[:, keys[h]], start=False, stop=False)
                for h in range(HALVES):
                    mm = pe.matmul(to[h], q_lo[:, query], k_hi[:, keys[h]], start=False, stop=True)
                mm.then_inc(s_scores, 1)

            def turn(b, i):
                pe.wait_ge(s_probs, BLOCKS * b + i + 1)
                for j in range(2):
                    wait(pe, s_pt_lo, 2 * (BLOCKS * b + i - 1) + j + 1)
                    for k in range(KB):
                        key = (j * KB + k) * 128
                        mm = pe.transpose(turned[:, j, k * 128:(k + 1) * 128],
                                          probs[:, i % RING, key:key + 128], ident[:, :])
                    mm.then_inc(s_turned, 1)

            def mix(b, g, chunk, bank=mixed):
                group = PAIR_GROUPS * b + g
                if chunk == 0 and bank is mixed:
                    wait(pe, s_result, group)
                    if not isinstance(b, int):
                        pe.wait_ge(s_norm, 3)
                if chunk % 2 == 0:
                    pe.wait_ge(s_pt_lo, 2 * (QB * group + QB - 1) + chunk // 2 + 1)
                    if g == 0:
                        pe.wait_ge(s_pj_lo, PJ * b + (VA, VB)[chunk // 2] + 1)
                for k in range(PAIR * chunk, PAIR * (chunk + 1)):
                    channels = slice(k * 128, (k + 1) * 128)
                    pe.matmul(bank[:, :], v_hi[:, channels], pt_hi[:, g, k, :], start=(k == 0), stop=False)
                    pe.matmul(bank[:, :], v_hi[:, channels], pt_lo[:, g, k, :], start=False, stop=False)
                    mm = pe.matmul(bank[:, :], v_lo[:, channels], pt_hi[:, g, k, :], start=False,
                                   stop=(k == BLOCKS - 1))
                mm.then_inc(s_mixed, 1)

            def keep_warm(count):
                for _ in range(count):
                    pe.matmul(scores[:, 0, 0:128], blank[:, :], blank[:, :], start=True, stop=True)

            pe.wait_ge(s_blank, 1)
            keep_warm(WARM[0])
            pe.wait_ge(s_const, 6 + GROUPS)
            group_means(0, 1, projected)
            keep_warm(WARM[1])
            group_variances(0, 1, projected)
            minus_group_means(0, 1, mixed)
            pe.wait_ge(s_w, 16)
            pe.wait_ge(s_vecs, 16)
            pe.matmul(scores[:, 1, 0:C], WV, WOUT_T, start=True, stop=True)
            pe.matmul(scores[:, 1, C:C + 1], WOUT_T, BV, start=True, stop=True).then_inc(s_wv, 1)
            keep_warm(WARM[2])
            pe.wait_ge(s_norm, 1)
            pe.wait_ge(s_w_lo, 2)
            halves = [slice(h * HALF, (h + 1) * HALF) for h in range(HALVES)]
            to = [bank[:, 0:HALF] for bank in FIRST_BANK]

            def head_products(p, w_hi, w_lo):
                pe.matmul(to[p], w_hi[:, :], y_hi[:, halves[p // 2]], start=True, stop=False)
                pe.matmul(to[p], w_lo[:, :], y_hi[:, halves[p // 2]], start=False, stop=False)

            def tail_product(p, w_hi):
                pe.matmul(to[p], w_hi[:, :], y_lo[:, halves[p // 2]], start=False, stop=True).then_inc(s_pj, 1)

            pe.wait_ge(s_y_hi_0, 1)
            head_products(K0, wk_hi, wk_lo)
            head_products(Q0, wq_hi, wq_lo)
            pe.wait_ge(s_y_lo_0a, 1)
            tail_product(K0, wk_hi)
            tail_product(Q0, wq_hi)
            pe.wait_ge(s_y_hi_0, 2)
            head_products(K1, wk_hi, wk_lo)
            pe.wait_ge(s_y_lo_0b, 1)
            tail_product(K1, wk_hi)
            head_products(Q1, wq_hi, wq_lo)
            tail_product(Q1, wq_hi)
            to = [scores[:, 0, half] for half in halves]
            query = slice(0, 128)
            pe.wait_ge(s_pj_hi, Q0 + 1)
            pe.matmul(to[0], q_hi[:, query], k_hi[:, halves[0]], start=True, stop=False)
            pe.wait_ge(s_pj_lo, K0 + 1)
            pe.matmul(to[0], q_hi[:, query], k_lo[:, halves[0]], start=False, stop=False)
            pe.wait_ge(s_pj_hi, K1 + 1)
            pe.matmul(to[1], q_hi[:, query], k_hi[:, halves[1]], start=True, stop=False)
            pe.wait_ge(s_pj_lo, Q0 + 1)
            pe.matmul(to[0], q_lo[:, query], k_hi[:, halves[0]], start=False, stop=True)
            pe.matmul(to[1], q_lo[:, query], k_hi[:, halves[1]], start=False, stop=False)
            group_means(1, 2, mixed, mixed)
            pe.wait_ge(s_pj_lo, K1 + 1)
            pe.matmul(to[1], q_hi[:, query], k_lo[:, halves[1]], start=False, stop=True).then_inc(s_scores, 1)
            pe.wait_ge(s_wv_out, 2)
            block_scores(0, 1)
            group_variances(1, 2, mixed)
            projection(0, VA)

            def steps(b, lo, hi, last=False, first=False):
                for i in range(lo, hi):
                    scored = (b, i + 2) if i + 2 < BLOCKS else (b + 1, i + 2 - BLOCKS)
                    ahead = i + 2 < BLOCKS or not last
                    if i == 6 and not last:
                        projection(b + 1, K1)
                    elif ahead:
                        block_scores(*scored)
                    if i == 5 and not last:
                        projection(b + 1, Q0)
                    if first and i == 0:
                        pe.wait_ge(s_pj_lo, Q1 + 1)
                    turn(b, i)
                    if first and i == 1:
                        pe.wait_ge(s_norm, 2)
                        group_means(2, BATCHES, mixed, mixed)
                    if first and i == 2:
                        group_variances(2, BATCHES, mixed)
                    if i == 2 and not first:
                        projection(b, VA)
                    if i in (4, 7) and not last:
                        projection(b + 1, {4: K0, 7: Q1}[i])
                    if i >= QB:
                        mix(b, 0, i - QB)
                    elif not first:
                        mix(b - 1, 1, i)
                    if i == 6 and ahead:
                        block_scores(*scored)
                    if i == 3:
                        projection(b, VB)

            steps(0, 0, QB, first=True)
            with pe.Fori(0, BATCHES - 1) as b:
                steps(b, QB, BLOCKS)
                steps(b + 1, 0, QB)
            steps(BATCHES - 1, QB, BLOCKS, last=True)
            for chunk in range(QB):
                mix(BATCHES - 1, 1, chunk, projected)


WARM = (10, 2, 4)
PAIR_GROUPS = 2


_N = 'L0_conv_'


def kernel(**inputs):
    import numpy as _np
    import concourse.bacc as _bacc
    from concourse import mybir as _mybir
    from concourse.bass_utils import run_bass_kernel_spmd as _run

    x = _np.ascontiguousarray(inputs['x'])
    c = x.shape[1]
    wq, wk, wv = _np.asarray(inputs[_N + 'w_qkv']).reshape(3, c, c)
    bq, bk, bv = _np.asarray(inputs[_N + 'b_qkv']).reshape(3, c)
    vectors = _np.ascontiguousarray(_np.stack(
        [inputs[_N + 'gn_gamma'], inputs[_N + 'gn_beta'], bq, bk, bv, inputs[_N + 'b_out']], axis=1))
    weights = _np.ascontiguousarray(_np.concatenate(
        [wq.T, wk.T, wv, _np.asarray(inputs[_N + 'w_out']).T], axis=1))

    nc = _bacc.Bacc("TRN2", target_bir_lowering=False, num_devices=1)
    arrays, args = {}, []
    for name, a in (("x", x), ("vectors", vectors), ("weights", weights)):
        arrays[f"in_{name}_dram"] = a
        args.append(nc.dram_tensor(f"in_{name}_dram", a.shape, _mybir.dt.from_np(a.dtype), kind="ExternalInput").ap())
    args.append(nc.dram_tensor("out_0_dram", x.shape, _mybir.dt.float32, kind="ExternalOutput").ap())
    attention_kernel(nc, *args)
    r = _run(nc, [arrays], core_ids=[0])
    return r.results[0]["out_0_dram"]
```
